# Optimizing a Trainium2 kernel written in Bass

```python
import numpy as np
import jax
import jax.numpy as jnp

def _softmax(x, axis=-1):
    return jax.nn.softmax(x, axis=axis)

def _gelu(x):
    return jax.nn.gelu(x, approximate=True)

def _silu(x):
    return jax.nn.silu(x)

def _sigmoid(x):
    return jax.nn.sigmoid(x)

def _layernorm(x, axis=-1, eps=1e-05):
    m = jnp.mean(x, axis=axis, keepdims=True)
    v = jnp.var(x, axis=axis, keepdims=True)
    return (x - m) / jnp.sqrt(v + eps)

def _scatter_add(tgt, idx, src, axis=0):
    return tgt.at[idx].add(src)

def _segment_sum(src, seg, n):
    return jax.ops.segment_sum(src, seg, n)
kernel_name = 'mk_flamingo_gated_d1_seqx_r8_0f966a'

def setup_inputs(seed: int=0):
    np.random.seed(seed)
    _w = jnp.asarray

    def _rec_inputs():
        import jax
        import jax.numpy as jnp
        _rk = jax.random.key(seed)
        x = -0.0002928 + 1 * jax.random.normal(jax.random.fold_in(_rk, 1), (8, 256, 128), jnp.float32)
        _lenS = 256 - jax.random.randint(jax.random.fold_in(_rk, 7), (8,), 0, max(1, 256 // 4) + 1, jnp.int32)
        _lenS2 = 64 - jax.random.randint(jax.random.fold_in(_rk, 8), (8,), 0, max(1, 64 // 4) + 1, jnp.int32)
        _ctx_1024P = jax.random.normal(jax.random.fold_in(_rk, 11), (8, 16, 128), jnp.float32)
        _ctx_1024c = jax.random.dirichlet(jax.random.fold_in(_rk, 511), 0.3 * jnp.ones((16,), jnp.float32), (8, 64))
        _ctx_1024t = jnp.einsum('bsk,bkd->bsd', _ctx_1024c, _ctx_1024P)
        _ctx_1024t = _ctx_1024t * jax.lax.rsqrt(jnp.mean(jnp.square(_ctx_1024t)) + 1e-12) * 0.953939
        ctx_1024 = 0.000227908 + 0.99994 * (_ctx_1024t + 0.3 * jax.random.normal(jax.random.fold_in(_rk, 611), (8, 64, 128), jnp.float32))
        _g = jax.random.normal(jax.random.fold_in(_rk, 9001), (2, 1), jnp.float32)
        _g = jnp.sign(_g) * jnp.maximum(jnp.abs(_g), 1.0) + (_g == 0) * 1.0
        g_xattn = _g[0]
        g_ffn = _g[1]
        return (x, ctx_1024, g_xattn, g_ffn)
    x, ctx_1024, g_xattn, g_ffn = _rec_inputs()

    def _L0_xattn_setup():
        import jax, jax.numpy as jnp
        import numpy as np
        HEADS = 16
        key = jax.random.key(seed)
        ks = jax.random.split(key, 6)
        b, n, m, dim = (2, 256, 64, 128)
        s = dim ** (-0.5)
        return {'x': jax.random.normal(ks[0], (b, n, dim), jnp.float32), 'mem': jax.random.normal(ks[1], (b, m, dim), jnp.float32), 'Wq': jax.random.normal(ks[2], (dim, dim), jnp.float32) * s, 'Wkv': jax.random.normal(ks[3], (dim, 2 * dim), jnp.float32) * s, 'Wout': jax.random.normal(ks[4], (dim, dim), jnp.float32) * s, 'bout': jnp.zeros((dim,), jnp.float32)}
    _L0_xattn_all = _L0_xattn_setup()
    _L0_xattn_in = {k: v for k, v in _L0_xattn_all.items() if k in ('Wq', 'Wkv', 'Wout', 'bout')}
    del _L0_xattn_all

    def _L0_ffn_setup():
        import jax, jax.numpy as jnp
        import numpy as np
        D = 128
        H = 512
        E = 8
        TOPK = 2
        CAP_F = 1.25
        key = jax.random.key(seed)
        ks = jax.random.split(key, 6)
        sc = 0.02
        return {'x': jax.random.normal(ks[0], (4, 256, D), jnp.float32), 'Wg': jax.random.normal(ks[1], (D, E), jnp.float32) * sc, 'bg': jnp.zeros((E,), jnp.float32), 'W1': jax.random.normal(ks[2], (E, D, H), jnp.float32) * sc, 'W2': jax.random.normal(ks[3], (E, D, H), jnp.float32) * sc, 'W3': jax.random.normal(ks[4], (E, H, D), jnp.float32) * sc}
    _L0_ffn_all = _L0_ffn_setup()
    _L0_ffn_in = {k: v for k, v in _L0_ffn_all.items() if k in ('Wg', 'bg', 'W1', 'W2', 'W3')}
    del _L0_ffn_all
    return {'x': x, 'ctx_1024': ctx_1024, 'g_xattn': g_xattn, 'g_ffn': g_ffn, 'L0_xattn_Wq': _L0_xattn_in['Wq'], 'L0_xattn_Wkv': _L0_xattn_in['Wkv'], 'L0_xattn_Wout': _L0_xattn_in['Wout'], 'L0_xattn_bout': _L0_xattn_in['bout'], 'L0_ffn_Wg': _L0_ffn_in['Wg'], 'L0_ffn_bg': _L0_ffn_in['bg'], 'L0_ffn_W1': _L0_ffn_in['W1'], 'L0_ffn_W2': _L0_ffn_in['W2'], 'L0_ffn_W3': _L0_ffn_in['W3']}

def reference(x, ctx_1024, g_xattn, g_ffn, L0_xattn_Wq, L0_xattn_Wkv, L0_xattn_Wout, L0_xattn_bout, L0_ffn_Wg, L0_ffn_bg, L0_ffn_W1, L0_ffn_W2, L0_ffn_W3):
    import jax
    import jax.numpy as jnp

    def _L0_xattn_ref(x, mem, Wq, Wkv, Wout, bout):
        import jax, jax.numpy as jnp
        import numpy as np
        HEADS = 16
        b, n, dim = x.shape
        h = HEADS
        d = dim // h
        scale = d ** (-0.5)
        mem_len = mem.shape[1]
        q = x @ Wq
        xc = jnp.concatenate((mem, x), axis=1)
        kv = xc @ Wkv
        k, v = jnp.split(kv, 2, axis=-1)

        def to_heads(t):
            bb, nn, _ = t.shape
            return t.reshape(bb, nn, h, d).transpose(0, 2, 1, 3)
        q, k, v = (to_heads(q), to_heads(k), to_heads(v))
        dots = jnp.einsum('bhid,bhjd->bhij', q, k) * scale
        j = dots.shape[-1]
        i_idx = jnp.arange(n)[:, None]
        j_idx = jnp.arange(j)[None, :]
        mask = j_idx > i_idx + mem_len
        dots = jnp.where(mask[None, None], -jnp.inf, dots)
        attn = jax.nn.softmax(dots, axis=-1)
        out = jnp.einsum('bhij,bhjd->bhid', attn, v)
        out = out.transpose(0, 2, 1, 3).reshape(b, n, dim)
        return out @ Wout + bout

    def _L0_ffn_ref(x, Wg, bg, W1, W2, W3):
        import jax, jax.numpy as jnp
        import numpy as np
        D = 128
        H = 512
        E = 8
        TOPK = 2
        CAP_F = 1.25
        b, s, d = x.shape
        xt = x.reshape(-1, d)
        T = xt.shape[0]
        capacity = int(T / E * CAP_F)
        gate_logits = xt @ Wg + bg
        top_v, top_i = jax.lax.top_k(gate_logits, TOPK)
        expert_label = jax.nn.one_hot(top_i, E, dtype=xt.dtype).sum(axis=1)
        seq = jnp.cumsum(expert_label, axis=0) * expert_label
        valid = (seq > 0) & (seq <= capacity)
        slot = (seq - 1.0).astype(jnp.int32)
        flat_idx = jnp.where(valid, jnp.arange(E, dtype=jnp.int32)[None, :] * capacity + slot, E * capacity)
        src = jnp.broadcast_to(xt[:, None, :], (T, E, d)).reshape(-1, d)
        buf = jnp.zeros((E * capacity + 1, d), xt.dtype).at[flat_idx.reshape(-1)].set(src)
        disp = buf[:-1].reshape(E, capacity, d)
        h = jax.nn.silu(jnp.einsum('ecd,edh->ech', disp, W1)) * jnp.einsum('ecd,edh->ech', disp, W2)
        out = jnp.einsum('ech,ehd->ecd', h, W3)
        out_flat = jnp.concatenate([out.reshape(E * capacity, d), jnp.zeros((1, d), xt.dtype)], axis=0)
        all_expert_output = out_flat[flat_idx]
        sel = jnp.take_along_axis(all_expert_output, top_i[:, :, None], axis=1)
        routing_w = jax.nn.softmax(top_v, axis=-1)
        y = (routing_w[:, :, None] * sel).sum(axis=1)
        return y.reshape(b, s, d)
    x = x + jnp.tanh(g_xattn[0]) * _L0_xattn_ref(_layernorm(x, axis=-1), ctx_1024, L0_xattn_Wq, L0_xattn_Wkv, L0_xattn_Wout, L0_xattn_bout)
    x = x + jnp.tanh(g_ffn[0]) * _L0_ffn_ref(_layernorm(x, axis=-1), L0_ffn_Wg, L0_ffn_bg, L0_ffn_W1, L0_ffn_W2, L0_ffn_W3)
    return x

_drawn_inputs = setup_inputs


def setup_inputs(seed=0):
    import zlib

    import numpy as np

    out = dict(_drawn_inputs(seed))
    spreads = {'L0_xattn_bout': (0.0, 0.1), 'L0_ffn_bg': (0.0, 0.8)}
    factors = {'L0_ffn_Wg': 8.0, 'L0_ffn_W1': 8.0, 'L0_ffn_W2': 8.0, 'L0_ffn_W3': 8.0}
    for name, (base, spread) in spreads.items():
        noise = np.random.default_rng([zlib.crc32(name.encode()), seed]).standard_normal(out[name].shape)
        drawn = base * np.exp(spread * noise) if base else spread * noise
        out[name] = jnp.asarray(drawn.astype(out[name].dtype))
    for name, factor in factors.items():
        out[name] = (out[name] * factor).astype(out[name].dtype)
    return out
```

```python
import concourse.bass as bass
from concourse import mybir
from contextlib import ExitStack


def flamingo_gated_block(nc, x, ctx, g_xattn, g_ffn, wq, wk, wv, wout, bout, wg, bg, w1, w2, w3,
                         slots_dram, answers_dram, out):
    fp32, bf16 = mybir.dt.float32, mybir.dt.bfloat16
    i32, u32 = mybir.dt.int32, mybir.dt.uint32
    ALU = mybir.AluOpType
    ACT = mybir.ActivationFunctionType
    AX = mybir.AxisListType

    B, N, D = x.shape
    M = ctx.shape[1]
    HEADS, HD = 16, 8
    PAIRS = HEADS // 2
    UP = 4
    UNITS = 2 * B
    KEYS = M + N
    T = B * N
    TILES = T // 128
    GROUPS = TILES // 4
    E, _, H = w1.shape
    HC = H // 128
    TOPK = 2
    CAP = int(T / E * 1.25)
    SLOTS = E * CAP
    ST_TILES = (CAP + 127) // 128
    LAST = CAP - 128 * (ST_TILES - 1)
    SCALE = float(HD) ** -0.5
    RING = 3
    QROW = 6 * HD
    MROW = 2 * QROW
    KROWS = MROW + 4
    QPART = (0, 0, 0, 1, 1, 2)
    KPART = (0, 1, 2, 0, 1, 0)
    VW = 32
    ROW = D + 2
    NEVER = 1 << 22
    MASKED = -1e30
    EPS = 1e-5

    es = ExitStack()
    with es:
        def sb(name, shape, dt=fp32):
            return es.enter_context(nc.sbuf_tensor(name, shape, dt))

        def sem(name):
            return es.enter_context(nc.semaphore(name))

        PS = es.enter_context(nc.psum_tensor("PS", [128, 8, 512], fp32))

        xs = sb("xs", [128, TILES, D])
        kst = sb("kst", [128, RING, PAIRS, 2, 2 * KEYS], bf16)
        qst = sb("qst", [128, RING, PAIRS, 2, N], bf16)
        pt = sb("pt", [128, 2, UP, 1024])
        vraw = sb("vraw", [128, B, 3, D])
        vp = sb("vp", [128, 2, 5 * PAIRS, VW])
        kp = sb("kp", [128, GROUPS, 3, 2, KEYS + M], bf16)
        qp = sb("qp", [128, GROUPS, 3, 512], bf16)
        w1s = sb("w1s", [128, 2, H])
        w2s = sb("w2s", [128, 2, H])
        w3s = sb("w3s", [128, 2, HC, D])
        wqs = sb("wqs", [128, D])
        wks = sb("wks", [128, D])
        wvs = sb("wvs", [128, D])
        wos = sb("wos", [128, 2, D])
        wgs = sb("wgs", [128, E])
        bg2 = sb("bg2", [128, 2, E])
        gx = sb("gx", [128, 1])
        gf = sb("gf", [128, 1])
        tgx = sb("tgx", [128, 1])
        tgf = sb("tgf", [128, 1])
        ident = sb("ident", [128, 128])
        identb = sb("identb", [128, 128], bf16)
        maskb = sb("maskb", [128, 2, 128], bf16)
        spread = sb("spread", [128, 128])
        tri = sb("tri", [128, 128], bf16)
        ones = sb("ones", [128, 128], bf16)
        half = sb("half", [128, 4])
        iotak = sb("iotak", [128, 4, E])
        dest_meta = sb("dest_meta", [128, TILES, 2], i32)
        blank = sb("blank", [128, ROW])
        stats = sb("stats", [128, 4, 6])
        mv = sb("mv", [128, 2, 4, 2])
        veps = sb("veps", [128, 2, 4])
        rstd = sb("rstd", [128, 2, 4])
        mx = sb("mx", [128, 2, 2, 2, UP])
        mrow = sb("mrow", [2 * UP, 2, 2, N], bf16)
        ots = sb("ots", [128, 2, N])
        rec = sb("rec", [128, N])
        att = sb("att", [128, 2, N])
        h2t = sb("h2t", [128, N])
        rows = sb("rows", [128, 2, TOPK, 2, ROW])
        lg = sb("lg", [128, 2, E])
        top = sb("top", [128, 2, 8])
        topi = sb("topi", [128, 2, 8], u32)
        idxf = sb("idxf", [128, 4])
        oh = sb("oh", [128, 4, E])
        lab = sb("lab", [128, 2, 2, E], bf16)
        run = sb("run", [128, 2, E], bf16)
        run1 = sb("run1", [128, E], bf16)
        d01 = sb("d01", [128, 2])
        e01 = sb("e01", [128, 2])
        s01 = sb("s01", [128, 2])
        ohp = sb("ohp", [128, 4, E])
        posk = sb("posk", [128, 4])
        over = sb("over", [128, 4])
        slotf = sb("slotf", [128, 4])
        dest = sb("dest", [128, 2, 4], u32)

        ptf = pt[:, :, :, :].rearrange("p a b c -> p (a b c)")
        zeros = ptf[:, 0:1024]
        xn = [ptf[:, 1024 + 512 * i:1536 + 512 * i].rearrange("p (t d) -> p t d", d=D) for i in range(2)]
        hT = [ptf[:, 2048 + 512 * i:2560 + 512 * i] for i in range(2)]
        ctxT = ptf[:, 3072:4096].rearrange("p (b c) -> p b c", c=128)
        ctxs = ptf[:, 4096:4608].rearrange("p (t d) -> p t d", d=D)
        rq = [ptf[:, 4608 + 512 * i:5120 + 512 * i] for i in range(2)]
        rk = [ptf[:, 5632 + 512 * i:6144 + 512 * i] for i in range(2)]

        kf = kst[:, :, :, :, :].rearrange("p a b c d -> p (a b c d)").bitcast(fp32)
        o = 0

        def room(n):
            nonlocal o
            o += n
            return kf[:, o - n:o]

        ex = room(E * ST_TILES * ROW).rearrange("p (e s c) -> p e s c", e=E, s=ST_TILES)
        xT = room(2 * CAP).rearrange("p (a c) -> p a c", a=2)
        gate = room(2 * CAP).rearrange("p (a c) -> p a c", a=2)
        hid = room(2 * HC * CAP).rearrange("p (a h c) -> p a h c", a=2, h=HC)
        yr = room(2 * ST_TILES * D).rearrange("p (a s d) -> p a s d", a=2, s=ST_TILES)
        qf = qst[:, :, :, :, :].rearrange("p a b c d -> p (a b c d)").bitcast(fp32)
        yy = qf[:, 0:TOPK * TILES * D].rearrange("p (k t d) -> p k t d", k=TOPK, t=TILES)

        w_in = sem("w_in")
        x_in = [sem(f"x_in{g}") for g in range(GROUPS)]
        ctx_in = sem("ctx_in")
        small_in = sem("small_in")
        zeroed = sem("zeroed")
        consts = sem("consts")
        cast = sem("cast")
        dram_zero = sem("dram_zero")
        stat = sem("stat")
        eps_added = sem("eps_added")
        rstd_ready = sem("rstd_ready")
        xn_ready = sem("xn_ready")
        tr_ready = sem("tr_ready")
        hT_ready = sem("hT_ready")
        q_ready = sem("q_ready")
        k_ready = sem("k_ready")
        v_ready = sem("v_ready")
        q1_done = sem("q1_done")
        k1_done = sem("k1_done")
        rq_done = sem("rq_done")
        rk_done = sem("rk_done")
        q2_done = sem("q2_done")
        k2_done = sem("k2_done")
        q3_done = sem("q3_done")
        k3_done = sem("k3_done")
        v_done = sem("v_done")
        stack_in = [sem(f"stack_in{g}") for g in range(GROUPS)]
        s_ready = sem("s_ready")
        max_done = sem("max_done")
        mT_ready = sem("mT_ready")
        mhi_done = sem("mhi_done")
        mlo_done = sem("mlo_done")
        m_in = [sem(f"m_in{i}") for i in range(2)]
        st_ready = sem("st_ready")
        exp_done = sem("exp_done")
        sel_done = sem("sel_done")
        vp_ready = sem("vp_ready")
        pv_done = sem("pv_done")
        ot_done = sem("ot_done")
        den_ready = sem("den_ready")
        rec_done = sem("rec_done")
        att_done = sem("att_done")
        y_ready = sem("y_ready")
        x1_done = sem("x1_done")
        tanh_done = sem("tanh_done")
        h2_ready = sem("h2_ready")
        h2T_ready = sem("h2T_ready")
        h2T_done = sem("h2T_done")
        row1_done = sem("row1_done")
        lg_ready = sem("lg_ready")
        route = sem("route")
        lab_ready = sem("lab_ready")
        d01_ready = sem("d01_ready")
        e01_done = sem("e01_done")
        pos_ready = sem("pos_ready")
        wts_done = sem("wts_done")
        dest_ready = sem("dest_ready")
        sent = [sem(f"sent{i}") for i in range(2)]
        wx_in = [sem(f"wx_in{i}") for i in range(2)]
        ex_in = [sem(f"ex_in{e}") for e in range(E)]
        xT_ready = sem("xT_ready")
        xT_done = sem("xT_done")
        h_ready = sem("h_ready")
        gate_done = sem("gate_done")
        hid_done = sem("hid_done")
        yo_ready = sem("yo_ready")
        yr_done = sem("yr_done")
        answered = [sem(f"answered{i}") for i in range(2)]
        yy_in = [sem(f"yy_in{g}") for g in range(GROUPS)]
        sum_done = sem("sum_done")
        out_done = sem("out_done")
        stored = sem("stored")

        S_ROUTE = 7
        S_WTS = 5
        S_STAT = 8
        MISC = PS[:, 7, 0:N]
        MT = PS[0:2 * UP, 7, N:2 * N]
        LOGITS = PS[:, 7, 0:2 * E].rearrange("p (t e) -> p t e", e=E)
        POS = PS[:, 7, 2 * E:4 * E].rearrange("p (t e) -> p t e", e=E)

        def O(U):
            return PS[:, (3, 6)[U % 2], 0:N]

        def place(U):
            b = U // 2
            return (b // 2) % RING, b % 2, UP * (U % 2)

        block = es.enter_context(nc.Block())

        @block.sync
        def _(sp):
            sp.dma_start(xs[:, 0:4, :], x_tiles(x)[:, 0:4, :]).then_inc(x_in[0], 16)
            for w, s in ((wq, wqs), (wk, wks), (wv, wvs)):
                sp.dma_start(s[:, :], w).then_inc(w_in, 16)
            for g in range(1, GROUPS):
                sp.dma_start(xs[:, 4 * g:4 * g + 4, :], x_tiles(x)[:, 4 * g:4 * g + 4, :]).then_inc(x_in[g], 16)

            def load_stack(g):
                s = g % RING
                sp.wait_ge(q3_done, g + 1)
                for par in range(2):
                    for r in range(6):
                        row = QROW * par + HD * r
                        sp.dma_start(qst[row:row + HD, s, :, :, :].rearrange("p g b n -> p g (b n)"),
                                     qp[64 * par:64 * par + 64, g, QPART[r], :]).then_inc(stack_in[g], 16)
                sp.wait_ge(k3_done, g + 2)
                for par in range(2):
                    for r in range(6):
                        row = QROW * par + HD * r
                        sp.dma_start(kst[row:row + HD, s, :, :, KEYS * par:KEYS * (par + 1)],
                                     kp[64 * par:64 * par + 64, g, KPART[r], :, M * (1 - par):M * (1 - par) + KEYS]).then_inc(stack_in[g], 16)

            def load_maxima(U):
                s, bb, g0 = place(U)
                sp.wait_ge(mhi_done, U + 1)
                sp.wait_ge(mlo_done, U + 1)
                for par in range(2):
                    for part in range(2):
                        row = MROW + 2 * par + part
                        sp.dma_start(qst[row:row + 1, s, g0:g0 + UP, bb, :],
                                     mrow[UP * par:UP * par + UP, U % 2, part, :]).then_inc(m_in[U % 2], 16)

            def load_expert(e):
                if e >= 2:
                    sp.wait_ge(yo_ready, e - 1)
                sp.dma_start(w1s[:, e % 2, :], w1[e]).then_inc(wx_in[e % 2], 16)
                sp.dma_start(w2s[:, e % 2, :], w2[e]).then_inc(wx_in[e % 2], 16)
                sp.dma_start(w3s[:, e % 2, :, :], w3[e].rearrange("(c p) d -> p c d", p=128)
                             ).then_inc(wx_in[e % 2], 16)

            sp.wait_ge(zeroed, 1)
            for g in range(RING):
                load_stack(g)
            for U in range(UNITS):
                load_maxima(U)
                if U == 4:
                    sp.wait_ge(st_ready, 4 * 2 * UP)
                    load_stack(RING)
                    load_expert(0)
                    load_expert(1)
            for i in range(2):
                sp.wait_ge(sent[i], 16 * 4 * B // 2)
            sp.wait_ge(st_ready, 2 * UP * UNITS)
            for e in range(E):
                r0 = e * CAP
                sp.dma_start(ex[:, e, 0:ST_TILES - 1, :],
                             slots_dram[r0:r0 + 128 * (ST_TILES - 1), :].rearrange("(s p) c -> p s c", p=128)
                             ).then_inc(ex_in[e], 16)
                sp.dma_start(ex[0:LAST, e, ST_TILES - 1, :],
                             slots_dram[r0 + 128 * (ST_TILES - 1):r0 + CAP, :]).then_inc(ex_in[e], 16)
            for e in range(2, E):
                load_expert(e)
            for i in range(2):
                sp.wait_ge(answered[i], 16 * ST_TILES * E // 2)
            av = answers_dram.rearrange("(k t p) d -> k p t d", k=TOPK, p=128)
            for g in range(GROUPS):
                for k in range(TOPK):
                    sp.dma_start(yy[:, k, 4 * g:4 * g + 4, :], av[k, :, 4 * g:4 * g + 4, :]).then_inc(yy_in[g], 16)
            for g in range(GROUPS):
                sp.wait_ge(out_done, g + 1)
                sp.dma_start(x_tiles(out)[:, 4 * g:4 * g + 4, :], xs[:, 4 * g:4 * g + 4, :]).then_inc(stored, 16)
            sp.wait_ge(stored, 16 * GROUPS)

        @block.gpsimd
        def _(pool):
            nc.gpsimd.memset(ident[:, :], 0.0).then_inc(consts, 1)
            pool.wait_ge(consts, 1)
            nc.gpsimd.affine_select(out=ident[:, :], in_=ident[:, :], compare_op=ALU.not_equal, fill=1.0, base=0,
                                    pattern=[[-1, 128]], channel_multiplier=1).then_inc(consts, 1)
            nc.gpsimd.memset(half[:, :], -0.5).then_inc(consts, 1)
            nc.gpsimd.memset(maskb[:, :, :], 0.0).then_inc(consts, 1)
            nc.gpsimd.memset(spread[:, :], 0.0).then_inc(consts, 1)
            nc.gpsimd.memset(ones[:, :], 1.0).then_inc(consts, 1)
            nc.gpsimd.memset(zeros, 0.0).then_inc(consts, 1)
            nc.gpsimd.memset(blank[:, :], 0.0).then_inc(consts, 1)
            pool.wait_ge(consts, 8)
            nc.gpsimd.affine_select(out=maskb[:, :, :], in_=maskb[:, :, :], compare_op=ALU.is_ge, fill=MASKED, base=0,
                                    pattern=[[0, 2], [-1, 128]], channel_multiplier=1).then_inc(consts, 1)
            sv = spread[:, :].rearrange("p (j r) -> p j r", j=UP)
            nc.gpsimd.affine_select(out=sv[:, :, 0:9], in_=sv[:, :, 0:9], compare_op=ALU.not_equal, fill=1.0, base=-8,
                                    pattern=[[-VW, UP], [0, 9]], channel_multiplier=1).then_inc(consts, 1)
            nc.gpsimd.affine_select(out=sv[:, :, 9:VW], in_=sv[:, :, 9:VW], compare_op=ALU.not_equal, fill=1.0,
                                    base=-17, pattern=[[-VW, UP], [0, VW - 9]],
                                    channel_multiplier=1).then_inc(consts, 1)
            nc.gpsimd.affine_select(out=tri[:, :], in_=ones[:, :], compare_op=ALU.is_ge, fill=0.0, base=0,
                                    pattern=[[1, 128]], channel_multiplier=-1).then_inc(consts, 1)
            nc.gpsimd.iota(iotak[:, :, :], pattern=[[0, 4], [1, E]], base=0, channel_multiplier=0,
                           allow_small_or_imprecise_dtypes=True).then_inc(consts, 1)
            nc.gpsimd.iota(dest_meta[:, :, :], pattern=[[128, TILES], [T, 2]], base=0,
                           channel_multiplier=1).then_inc(consts, 1)
            nc.gpsimd.iota(blank[:, D:D + 1].bitcast(i32), pattern=[[0, 1]], base=NEVER,
                           channel_multiplier=0).then_inc(consts, 1)

            pool.wait_ge(consts, 15)
            av = answers_dram.rearrange("(z p n) d -> z p (n d)", z=4, p=128)
            for z in range(4):
                nc.gpsimd.dma_start(av[z], zeros).then_inc(dram_zero, 16)
            bv = blank[:, :]
            nc.gpsimd.dma_start(slots_dram.rearrange("(n p) c -> p n c", p=128),
                                bass.AP(tensor=bv.tensor, offset=bv.offset,
                                        ap=[bv.ap[0], [0, SLOTS // 128], [1, ROW]])).then_inc(dram_zero, 16)

            def rstd_of(n, par, count, stats_by):
                pool.wait_ge(stat, stats_by)
                nc.gpsimd.tensor_scalar(veps[:, par, 0:count], mv[:, par, 0:count, 1], 1.0, EPS, ALU.mult,
                                        ALU.add).then_inc(eps_added, 1)
                pool.wait_ge(eps_added, n + 1)
                nc.gpsimd.tensor_tensor(rstd[:, par, 0:count], veps[:, par, 0:count], half[:, 0:count],
                                        ALU.pow).then_inc(rstd_ready, 1)

            for g in range(GROUPS):
                rstd_of(g, g % 2, 4, S_STAT * (g + 1))
            for U in range(UNITS + 6):
                if U < UNITS:
                    for g in range(UP):
                        pool.wait_ge(exp_done, 2 * (UP * U + g + 1))
                        v = pt[:, U % 2, g, :].rearrange("p (s c) -> p s c", s=4)[:, :, 0:128]
                        nc.gpsimd.affine_select(out=v, in_=v, compare_op=ALU.is_ge, fill=0.0, base=0,
                                                pattern=[[0, 4], [1, 128]],
                                                channel_multiplier=-1).then_inc(sel_done, 1)
                if U % 2 and U >= 3 and (U - 3) // 2 < B:
                    b = (U - 3) // 2
                    rstd_of(GROUPS + b, b % 2, 2, S_STAT * GROUPS + 4 * (b + 1))
                if U % 2 == 0 and 0 <= (U - 6) // 2 < B:
                    b = (U - 6) // 2
                    if b == 0:
                        pool.wait_ge(dram_zero, 16 * 5)
                    pool.wait_ge(dest_ready, b + 1)
                    pool.wait_ge(row1_done, b + 1)
                    for k in range(TOPK):
                        for t in range(2):
                            nc.gpsimd.indirect_dma_start(
                                out=slots_dram, out_offset=bass.IndirectOffsetOnAxis(
                                    ap=dest[:, b % 2, 2 * t + k:2 * t + k + 1], axis=0),
                                in_=rows[:, b % 2, k, t, :], in_offset=None,
                                bounds_check=SLOTS - 1, oob_is_err=False).then_inc(sent[b % 2], 16)
            for e in range(E):
                pool.wait_ge(yr_done, e + 1)
                for s in range(ST_TILES):
                    n = 128 if s < ST_TILES - 1 else LAST
                    nc.gpsimd.indirect_dma_start(
                        out=answers_dram, out_offset=bass.IndirectOffsetOnAxis(
                            ap=ex[0:n, e, s, D:D + 1].bitcast(u32), axis=0),
                        in_=yr[0:n, e % 2, s, :], in_offset=None,
                        bounds_check=TOPK * T - 1, oob_is_err=False).then_inc(answered[e % 2], 16)

        @block.scalar
        def _(act):
            act.dma_start(ctxs, ctx.rearrange("b m d -> (b m) d").rearrange("(t p) d -> p t d", p=128)
                          ).then_inc(ctx_in, 16)
            act.dma_start(gx[:, :], g_xattn.partition_broadcast(128)).then_inc(small_in, 16)
            act.dma_start(gf[:, :], g_ffn.partition_broadcast(128)).then_inc(small_in, 16)
            act.dma_start(wgs[:, :], wg).then_inc(small_in, 16)
            for t in range(2):
                act.dma_start(bg2[:, t, :], bg.partition_broadcast(128)).then_inc(small_in, 16)
            act.wait_ge(zeroed, 1)
            for u in range(2):
                for j in range(UP):
                    for par in range(2):
                        src = (2 * (UP * u + j) + par) * HD
                        act.dma_start(wos[VW * j + 9 * par:VW * j + 9 * par + HD, u, :],
                                      wout[src:src + HD, :]).then_inc(small_in, 16)
            act.dma_start(wos[HD:HD + 1, 0, :], bout.rearrange("(a n) -> a n", a=1)).then_inc(small_in, 16)

            def part1(dst, src):
                return nc.scalar.copy(dst, src)

            act.wait_ge(tr_ready, 1)
            v = PS[:, 0, :].rearrange("p (b m) -> p b m", m=M)
            nc.scalar.copy(ctxT[:, :, 0:M], v)
            nc.scalar.copy(ctxT[:, :, M:2 * M], v).then_inc(hT_ready, 1)
            act.wait_ge(k_ready, 1)
            kc = PS[:, 4, :].rearrange("p (g b m) -> p g b m", g=GROUPS, b=2)
            nc.scalar.copy(kp[:, :, 0, :, 0:M], kc).then_inc(k1_done, 1)
            act.wait_ge(rk_done, 1)
            nc.scalar.copy(kp[:, :, 1, :, 0:M], rk[0].rearrange("p (g b m) -> p g b m", g=GROUPS, b=2)
                           ).then_inc(k2_done, 1)
            for g in range(GROUPS):
                i = (g + 1) % 2
                act.wait_ge(tr_ready, g + 2)
                if g >= 2:
                    act.wait_ge(v_ready, g)
                nc.scalar.copy(hT[g % 2], PS[:, i, :]).then_inc(hT_ready, 1)
                act.wait_ge(q_ready, g + 1)
                nc.scalar.copy(qp[:, g, 0, :], PS[:, 2 + i, :]).then_inc(q1_done, 1)
                act.wait_ge(k_ready, g + 2)
                nc.scalar.copy(kp[:, g, 0, :, M:KEYS], PS[:, 4 + i, :].rearrange("p (b n) -> p b n", b=2)
                               ).then_inc(k1_done, 1)
                act.wait_ge(rq_done, g + 1)
                nc.scalar.copy(qp[:, g, 1, :], rq[g % 2]).then_inc(q2_done, 1)
                act.wait_ge(rk_done, g + 2)
                nc.scalar.copy(kp[:, g, 1, :, M:KEYS], rk[i].rearrange("p (b n) -> p b n", b=2)
                               ).then_inc(k2_done, 1)
            act.wait_ge(small_in, 16 * 22)
            nc.scalar.activation(tgx[:, :], gx[:, :], ACT.Tanh)
            nc.scalar.activation(tgf[:, :], gf[:, :], ACT.Tanh).then_inc(tanh_done, 1)

            def maxima_row(U):
                act.wait_ge(mT_ready, U + 1)
                if U >= 2:
                    act.wait_ge(m_in[U % 2], 64 * (U // 2))
                nc.scalar.copy(mrow[:, U % 2, 0, :], MT).then_inc(mhi_done, 1)

            def pad_values(b):
                if b == 0:
                    act.wait_ge(v_done, GROUPS + 1)
                if b >= 2:
                    act.wait_ge(pv_done, 2 * b - 2)
                for par in range(2):
                    lo = vraw[64 * par:64 * par + 64, b, 0, :].rearrange("p (g q d) -> p g q d", q=2, d=HD)
                    c0 = 9 * par
                    nc.scalar.copy(vp[64 * par:64 * par + 64, b % 2, 0:PAIRS, c0:c0 + HD], lo[:, :, par, :])
                    for blk in range(2):
                        dst = vp[:, b % 2, PAIRS * (1 + 2 * blk):PAIRS * (3 + 2 * blk), :].rearrange(
                            "p (g q) c -> p g q c", q=2)
                        src = vraw[:, b, 1 + blk, :].rearrange("p (g q d) -> p g q d", q=2, d=HD)
                        ins = nc.scalar.copy(dst[:, :, par, c0:c0 + HD], src[:, :, par, :])
                ins.then_inc(vp_ready, 1)

            maxima_row(0)
            for U in range(UNITS + 6):
                if U >= 2 and U - 2 < UNITS:
                    V = U - 2
                    act.wait_ge(pv_done, V + 1)
                    if V >= 2:
                        act.wait_ge(att_done, V - 1)
                    nc.scalar.copy(ots[:, V % 2, :], O(V)).then_inc(ot_done, 1)
                for g in range(UP):
                    if U < UNITS:
                        if U == 0 and g == 0:
                            act.wait_ge(dram_zero, 16 * 5)
                            act.wait_ge(q3_done, GROUPS)
                            act.wait_ge(k3_done, GROUPS + 1)
                            act.wait_ge(v_ready, GROUPS + 1)
                        if U >= 2 and g == 0:
                            act.wait_ge(pv_done, U - 1)
                        for par in range(2):
                            n = 2 * (UP * U + g) + par
                            act.wait_ge(st_ready, n + 1)
                            nc.scalar.activation(pt[:, U % 2, g, 512 * par:512 * par + 512], PS[:, n % 3, :],
                                                 ACT.Exp, scale=SCALE).then_inc(exp_done, 1)
                    if g == 0 and U + 1 < UNITS:
                        maxima_row(U + 1)
                    if g == 1 and U % 2 == 0 and U // 2 < B:
                        pad_values(U // 2)
                    if g == 2 and U % 2 == 0 and 0 <= (U - 4) // 2 < B:
                        b = (U - 4) // 2
                        act.wait_ge(h2T_ready, b + 1)
                        nc.scalar.copy(h2t[:, :], MISC).then_inc(h2T_done, 1)
                        if b >= 2:
                            act.wait_ge(sent[b % 2], 16 * 4 * (b // 2))
                        nc.scalar.copy(rows[:, b % 2, 1, :, 0:D], rows[:, b % 2, 0, :, 0:D]).then_inc(row1_done, 1)
                    if g == 1 and U % 2 and 0 <= (U - 5) // 2 < B:
                        b = (U - 5) // 2
                        act.wait_ge(d01_ready, b + 1)
                        nc.scalar.activation(e01[:, :], d01[:, :], ACT.Exp).then_inc(e01_done, 1)

            def tokens_in(e):
                act.wait_ge(xT_ready, e + 1)
                if e >= 2:
                    act.wait_ge(h_ready, HC * (e - 1))
                nc.scalar.copy(xT[:, e % 2, :], PS[:, e % 2, 0:CAP]).then_inc(xT_done, 1)

            tokens_in(0)
            for e in range(E):
                for c in range(HC):
                    n = HC * e + c
                    act.wait_ge(h_ready, n + 1)
                    if n >= 2:
                        act.wait_ge(hid_done, n - 1)
                    nc.scalar.activation(gate[:, n % 2, :], PS[:, 2 + n % 2, 0:CAP], ACT.Silu).then_inc(gate_done, 1)
                if e + 1 < E:
                    tokens_in(e + 1)

        @block.vector
        def _(dve):
            nc.vector.memset(wos[:, :, :], 0.0)
            for s in range(RING):
                v = kst[0:MROW, s, :, :, :].rearrange("p g b k -> p (g b k)").bitcast(fp32)
                nc.vector.memset(v, 0.0)
            fixed = kst[:, :, :, :, :].rearrange("p s g b k -> p (s g b) k")
            nc.vector.memset(fixed[MROW:KROWS, :, 0:KEYS], 0.0).then_inc(cast, 1)
            nc.vector.memset(fixed[MROW:KROWS, :, KEYS:2 * KEYS], -1.0).then_inc(cast, 1)
            dve.wait_ge(cast, 2)
            nc.vector.memset(fixed[MROW:MROW + 2, :, 0:KEYS], -1.0)
            nc.vector.memset(fixed[MROW:MROW + 2, :, KEYS:2 * KEYS], 0.0).then_inc(zeroed, 1)


            def norm_tokens(g):
                dve.wait_ge(rstd_ready, g + 1)
                if g >= 2:
                    dve.wait_ge(tr_ready, g)
                for i in range(4):
                    c = nc.vector.tensor_scalar(xn[g % 2][:, i, :], xs[:, 4 * g + i, :], mv[:, g % 2, i, 0:1],
                                                rstd[:, g % 2, i:i + 1], ALU.subtract, ALU.mult)
                c.then_inc(xn_ready, 1)

            def ctx_parts():
                dve.wait_ge(k1_done, 1)
                kc = PS[:, 4, :].rearrange("p (g b m) -> p g b m", g=GROUPS, b=2)
                rv = rk[0].rearrange("p (g b m) -> p g b m", g=GROUPS, b=2)
                nc.vector.tensor_tensor(rv, kc, kp[:, :, 0, :, 0:M], ALU.subtract).then_inc(rk_done, 1)
                dve.wait_ge(k2_done, 1)
                nc.vector.tensor_tensor(kp[:, :, 2, :, 0:M], rv, kp[:, :, 1, :, 0:M], ALU.subtract
                                        ).then_inc(cast, 1)
                dve.wait_ge(cast, 3)
                allp = kp[:, :, :, :, :].rearrange("p g c b k -> p (g c b) k")
                nc.vector.tensor_copy(allp[:, :, KEYS:KEYS + M], allp[:, :, 0:M]).then_inc(k3_done, 1)
                dve.wait_ge(v_ready, 1)
                nc.vector.tensor_copy(vraw[:, 0:4, 0, :], PS[:, 6, :].rearrange("p (b d) -> p b d", d=D))
                nc.vector.tensor_copy(vraw[:, 4:8, 0, :], PS[:, 2, :].rearrange("p (b d) -> p b d", d=D)
                                      ).then_inc(v_done, 1)

            def parts(g):
                i = (g + 1) % 2
                dve.wait_ge(q1_done, g + 1)
                nc.vector.tensor_tensor(rq[g % 2], PS[:, 2 + i, :], qp[:, g, 0, :], ALU.subtract
                                        ).then_inc(rq_done, 1)
                dve.wait_ge(k1_done, g + 2)
                kv = rk[i].rearrange("p (b n) -> p b n", b=2)
                nc.vector.tensor_tensor(kv, PS[:, 4 + i, :].rearrange("p (b n) -> p b n", b=2),
                                        kp[:, g, 0, :, M:KEYS], ALU.subtract).then_inc(rk_done, 1)
                dve.wait_ge(v_ready, g + 2)
                nc.vector.tensor_copy(vraw[:, 2 * g:2 * g + 2, 1:3, :],
                                      PS[:, 6 + i, :].rearrange("p (b t d) -> p b t d", b=2, t=2)
                                      ).then_inc(v_done, 1)
                dve.wait_ge(q2_done, g + 1)
                nc.vector.tensor_tensor(qp[:, g, 2, :], rq[g % 2], qp[:, g, 1, :], ALU.subtract
                                        ).then_inc(q3_done, 1)
                dve.wait_ge(k2_done, g + 2)
                nc.vector.tensor_tensor(kp[:, g, 2, :, M:KEYS], kv, kp[:, g, 1, :, M:KEYS], ALU.subtract
                                        ).then_inc(k3_done, 1)

            def stats_group(g):
                dve.wait_ge(x_in[g], 16)
                if g >= 1:
                    dve.wait_ge(stat, S_STAT * g)
                for i in range(4):
                    nc.vector.bn_stats(stats[:, i, :], xs[:, 4 * g + i, :]).then_inc(stat, 1)
                for i in range(4):
                    dve.wait_ge(stat, S_STAT * g + i + 1)
                    nc.vector.bn_aggr(mv[:, g % 2, i, :], stats[:, i, :]).then_inc(stat, 1)

            stats_group(0)
            norm_tokens(0)
            ctx_parts()
            for g in range(GROUPS):
                if g + 1 < GROUPS:
                    stats_group(g + 1)
                    norm_tokens(g + 1)
                parts(g)
            nc.vector.memset(vp[:, :, :, :].rearrange("p a b c -> p (a b c)"), 0.0).then_inc(cast, 1)
            dve.wait_ge(cast, 4)
            nc.vector.memset(vp[0:64, :, 0:PAIRS, 8:9], 1.0)
            nc.vector.memset(vp[64:128, :, 0:PAIRS, 17:18], 1.0)
            for par in range(2):
                v = vp[:, :, PAIRS:5 * PAIRS, :].rearrange("p a (g q) c -> p a g q c", q=2)
                nc.vector.memset(v[:, :, :, par, 8 + 9 * par:9 + 9 * par], 1.0)
            dve.wait_ge(consts, 15)
            nc.vector.tensor_copy(identb[:, :], ident[:, :])
            nc.vector.memset(run[:, 0, :], 0.0).then_inc(cast, 1)

            def maxima(U, g):
                n = 3 * (UP * U + g)
                if g == 0 and U >= 2:
                    dve.wait_ge(mT_ready, U - 1)
                dve.wait_ge(s_ready, n + 1)
                nc.vector.tensor_reduce(mx[:, U % 2, 0, :, g],
                                        PS[:, 4 + n % 2, 0:2 * (M + 128)].rearrange("p (q k) -> p q k", q=2),
                                        axis=AX.X, op=ALU.max).then_inc(max_done, 1)
                for par in range(2):
                    n += 1
                    dve.wait_ge(s_ready, n + 1)
                    nc.vector.tensor_reduce(mx[:, U % 2, 1, par, g:g + 1], PS[:, 4 + n % 2, 0:KEYS],
                                            axis=AX.X, op=ALU.max).then_inc(max_done, 1)

            def maxima_rest(U):
                dve.wait_ge(mhi_done, U + 1)
                nc.vector.tensor_tensor(mrow[:, U % 2, 1, :], MT, mrow[:, U % 2, 0, :], ALU.subtract
                                        ).then_inc(mlo_done, 1)

            def normalize(V):
                dve.wait_ge(den_ready, V + 1)
                nc.vector.reciprocal(rec[:, :], MISC).then_inc(rec_done, 1)
                dve.wait_ge(rec_done, V + 1)
                if V >= 2:
                    dve.wait_ge(y_ready, V // 2)
                nc.vector.tensor_tensor(att[:, V % 2, :], ots[:, V % 2, :], rec[:, :], ALU.mult
                                        ).then_inc(att_done, 1)

            def tokens_norm(b):
                base = S_STAT * GROUPS + 4 * b
                dve.wait_ge(y_ready, b + 1)
                if b == 0:
                    dve.wait_ge(tanh_done, 1)
                v = xs[:, 2 * b:2 * b + 2, :]
                nc.vector.scalar_tensor_tensor(v, MISC.rearrange("p (t d) -> p t d", t=2), tgx[:, 0:1], v,
                                               ALU.mult, ALU.add).then_inc(x1_done, 1)
                dve.wait_ge(x1_done, b + 1)
                dve.wait_ge(stat, base)
                for i in range(2):
                    nc.vector.bn_stats(stats[:, i, :], xs[:, 2 * b + i, :]).then_inc(stat, 1)
                for i in range(2):
                    dve.wait_ge(stat, base + i + 1)
                    nc.vector.bn_aggr(mv[:, b % 2, i, :], stats[:, i, :]).then_inc(stat, 1)

            def tokens_out(b):
                dve.wait_ge(rstd_ready, GROUPS + b + 1)
                if b >= 2:
                    dve.wait_ge(sent[b % 2], 16 * 4 * (b // 2))
                    dve.wait_ge(row1_done, b - 1)
                for i in range(2):
                    c = nc.vector.tensor_scalar(rows[:, b % 2, 0, i, 0:D], xs[:, 2 * b + i, :], mv[:, b % 2, i, 0:1],
                                                rstd[:, b % 2, i:i + 1], ALU.subtract, ALU.mult)
                c.then_inc(h2_ready, 1)

            def top_two(b):
                r = S_ROUTE * b
                dve.wait_ge(lg_ready, b + 1)
                nc.vector.tensor_tensor(lg[:, :, :], LOGITS, bg2[:, :, :], ALU.add).then_inc(route, 1)
                dve.wait_ge(route, r + 1)
                for t in range(2):
                    c = nc.vector.max(top[:, t, :], lg[:, t, :])
                c.then_inc(route, 1)
                dve.wait_ge(route, r + 2)
                for t in range(2):
                    c = nc.vector.max_index(topi[:, t, :], top[:, t, :], lg[:, t, :])
                c.then_inc(route, 1)
                nc.vector.tensor_tensor(d01[:, :], top[:, :, 1], top[:, :, 0], ALU.subtract).then_inc(d01_ready, 1)
                dve.wait_ge(route, r + 3)
                if b >= 1:
                    dve.wait_ge(dest_ready, b)
                nc.vector.tensor_copy(idxf[:, :].rearrange("p (t k) -> p t k", t=2), topi[:, :, 0:TOPK]
                                      ).then_inc(route, 1)
                dve.wait_ge(route, r + 4)
                iv = idxf[:, :]
                nc.vector.tensor_tensor(oh[:, :, :], iotak[:, :, :],
                                        bass.AP(tensor=iv.tensor, offset=iv.offset, ap=[iv.ap[0], [1, 4], [0, E]]),
                                        ALU.is_equal).then_inc(route, 1)
                dve.wait_ge(route, r + 5)
                ov = oh[:, :, :].rearrange("p (t k) e -> p t k e", k=TOPK)
                if b >= 2:
                    dve.wait_ge(pos_ready, b - 1)
                nc.vector.tensor_tensor(lab[:, b % 2, :, :], ov[:, :, 0, :], ov[:, :, 1, :], ALU.add
                                        ).then_inc(lab_ready, 1)
                dve.wait_ge(lab_ready, b + 1)
                nc.vector.tensor_tensor(run1[:, :], run[:, b % 2, :], lab[:, b % 2, 0, :], ALU.add).then_inc(route, 1)
                dve.wait_ge(route, r + 6)
                if b >= 1:
                    dve.wait_ge(pos_ready, b)
                nc.vector.tensor_tensor(run[:, (b + 1) % 2, :], run1[:, :], lab[:, b % 2, 1, :], ALU.add
                                        ).then_inc(route, 1)

            def destinations(b):
                dve.wait_ge(e01_done, b + 1)
                wr = S_WTS * b
                nc.vector.tensor_scalar(s01[:, :], e01[:, :], 1.0, None, ALU.add).then_inc(wts_done, 1)
                dve.wait_ge(wts_done, wr + 1)
                nc.vector.reciprocal(rows[:, b % 2, 0, :, D + 1], s01[:, :]).then_inc(wts_done, 1)
                dve.wait_ge(wts_done, wr + 2)
                nc.vector.tensor_tensor(rows[:, b % 2, 1, :, D + 1], rows[:, b % 2, 0, :, D + 1], e01[:, :], ALU.mult)
                for k in range(TOPK):
                    nc.vector.tensor_copy(rows[:, b % 2, k, :, D].bitcast(i32), dest_meta[:, 2 * b:2 * b + 2, k])
                dve.wait_ge(pos_ready, b + 1)
                pv = POS
                nc.vector.tensor_tensor(ohp[:, :, :].rearrange("p (t k) e -> p t k e", k=TOPK),
                                        bass.AP(tensor=pv.tensor, offset=pv.offset,
                                                ap=[pv.ap[0], [E, 2], [0, TOPK], [1, E]]),
                                        oh[:, :, :].rearrange("p (t k) e -> p t k e", k=TOPK),
                                        ALU.mult).then_inc(wts_done, 1)
                dve.wait_ge(wts_done, wr + 3)
                nc.vector.tensor_reduce(posk[:, :], ohp[:, :, :], axis=AX.X, op=ALU.add).then_inc(wts_done, 1)
                dve.wait_ge(wts_done, wr + 4)
                nc.vector.tensor_scalar(over[:, :], posk[:, :], float(CAP), float(NEVER), ALU.is_gt, ALU.mult)
                nc.vector.scalar_tensor_tensor(slotf[:, :], idxf[:, :], float(CAP), posk[:, :], ALU.mult, ALU.add
                                               ).then_inc(wts_done, 1)
                dve.wait_ge(wts_done, wr + 5)
                nc.vector.scalar_tensor_tensor(dest[:, b % 2, :], slotf[:, :], -1.0, over[:, :], ALU.add, ALU.add
                                               ).then_inc(dest_ready, 1)

            for U in range(-2, UNITS + 6):
                for g in range(UP):
                    if U + 2 < UNITS:
                        maxima(U + 2, g)
                    if g == 0 and U % 2 and 0 <= (U - 5) // 2 < B:
                        top_two((U - 5) // 2)
                    if g == 0 and -1 <= U and U + 1 < UNITS:
                        maxima_rest(U + 1)
                    if g == 1 and 0 <= U - 2 < UNITS:
                        normalize(U - 2)
                    if U % 2 and U >= 3 and (U - 3) // 2 < B:
                        if g == 2:
                            tokens_norm((U - 3) // 2)
                        if g == 3:
                            tokens_out((U - 3) // 2)
                    if g == 3 and U % 2 and 0 <= (U - 5) // 2 < B:
                        destinations((U - 5) // 2)

            for e in range(E):
                for c in range(HC):
                    n = HC * e + c
                    dve.wait_ge(gate_done, n + 1)
                    if e >= 2 and c == 0:
                        dve.wait_ge(yo_ready, e - 1)
                    nc.vector.tensor_tensor(hid[:, e % 2, c, :], PS[:, 4 + n % 2, 0:CAP], gate[:, n % 2, :],
                                            ALU.mult).then_inc(hid_done, 1)
                dve.wait_ge(yo_ready, e + 1)
                if e >= 2:
                    dve.wait_ge(answered[e % 2], 16 * ST_TILES * (e // 2))
                for s in range(ST_TILES):
                    n = 128 if s < ST_TILES - 1 else LAST
                    c = nc.vector.tensor_scalar(yr[0:n, e % 2, s, :], PS[0:n, 6 + e % 2, 128 * s:128 * s + D],
                                                ex[0:n, e, s, D + 1:D + 2], None, ALU.mult)
                c.then_inc(yr_done, 1)
            for g in range(GROUPS):
                v = yy[:, 0, 4 * g:4 * g + 4, :]
                dve.wait_ge(yy_in[g], 32)
                nc.vector.tensor_tensor(v, v, yy[:, 1, 4 * g:4 * g + 4, :], ALU.add).then_inc(sum_done, 1)
                dve.wait_ge(sum_done, g + 1)
                xv = xs[:, 4 * g:4 * g + 4, :]
                nc.vector.scalar_tensor_tensor(xv, v, tgf[:, 0:1], xv, ALU.mult, ALU.add).then_inc(out_done, 1)

        @block.tensor
        def _(pe):
            def transpose4(src, bank):
                for i in range(4):
                    c = nc.tensor.transpose(PS[:, bank, 128 * i:128 * i + 128], src[:, i, :], ident[:, :])
                c.then_inc(tr_ready, 1)

            pe.wait_ge(consts, 2)
            pe.wait_ge(ctx_in, 16)
            transpose4(ctxs, 0)
            pe.wait_ge(w_in, 48)
            pe.wait_ge(hT_ready, 1)
            nc.tensor.matmul(PS[:, 4, :].rearrange("p (b m) -> p b m", m=M), wks[:, :], ctxT[:, :, 0:M],
                             start=True, stop=True).then_inc(k_ready, 1)
            for b in range(B):
                c = nc.tensor.matmul(PS[:, 6 if b < 4 else 2, 128 * (b % 4):128 * (b % 4) + 128], ctxT[:, b, :],
                                     wvs[:, :], start=True, stop=True)
            c.then_inc(v_ready, 1)
            for g in range(GROUPS):
                i = (g + 1) % 2
                pe.wait_ge(xn_ready, g + 1)
                transpose4(xn[g % 2], i)
                pe.wait_ge(hT_ready, g + 2)
                if g == 1:
                    pe.wait_ge(v_done, 1)
                if g >= 2:
                    pe.wait_ge(rq_done, g - 1)
                nc.tensor.matmul(PS[:, 2 + i, :], wqs[:, :], hT[g % 2], start=True, stop=True).then_inc(q_ready, 1)
                if g >= 1:
                    pe.wait_ge(rk_done, g)
                nc.tensor.matmul(PS[:, 4 + i, :], wks[:, :], hT[g % 2], start=True, stop=True).then_inc(k_ready, 1)
                if g >= 1:
                    pe.wait_ge(v_done, g)
                for t in range(4):
                    c = nc.tensor.matmul(PS[:, 6 + i, 128 * t:128 * t + 128], hT[g % 2][:, 128 * t:128 * t + 128],
                                         wvs[:, :], start=True, stop=True)
                c.then_inc(v_ready, 1)

            def scores(U, g):
                s, bb, g0 = place(U)
                if g == 0 and U % 4 == 0:
                    pe.wait_ge(stack_in[U // 4], 16 * 24)
                n = 3 * (UP * U + g)
                for piece in range(3):
                    if n >= 2:
                        pe.wait_ge(max_done, n - 1)
                    bank = PS[:, 4 + n % 2, :]
                    if piece == 0:
                        q = qst[0:MROW, s, g0 + g, bb, 0:128]
                        nc.tensor.matmul(bank[:, 0:128], q, kst[0:MROW, s, g0 + g, bb, 0:128], start=True, stop=False)
                        nc.tensor.matmul(bank[:, 128:384], q, kst[0:MROW, s, g0 + g, bb, N:2 * N],
                                         start=False, stop=False)
                        c = nc.tensor.matmul(bank[:, 0:512].rearrange("p (q k) -> p q k", q=2)[:, :, 0:128],
                                             identb[:, :], maskb[:, :, :], start=False, stop=True)
                    else:
                        par = piece - 1
                        own = 128 + M * par
                        nc.tensor.matmul(bank[:, 0:KEYS], qst[0:MROW, s, g0 + g, bb, 128:256],
                                         kst[0:MROW, s, g0 + g, bb, KEYS * par:KEYS * (par + 1)],
                                         start=True, stop=False)
                        c = nc.tensor.matmul(bank[:, own:own + 128], identb[:, :], maskb[:, 0, :],
                                             start=False, stop=True)
                    c.then_inc(s_ready, 1)
                    n += 1

            def scores_t(U, g):
                s, bb, g0 = place(U)
                if g == 0:
                    pe.wait_ge(m_in[U % 2], 64 * (U // 2 + 1))
                q = qst[0:KROWS, s, g0 + g, bb, :]
                k = kst[0:KROWS, s, g0 + g, bb, :]
                odd = N + 2 * M
                for par, k0 in ((0, 0), (1, odd)):
                    n = 2 * (UP * U + g) + par
                    if n >= 3:
                        pe.wait_ge(exp_done, n - 2)
                    nc.tensor.matmul(PS[:, n % 3, 0:N], k[:, k0:k0 + 128], q, start=True, stop=True)
                    nc.tensor.matmul(PS[:, n % 3, N:N + 128], k[:, k0 + 128:k0 + N], q[:, 128:N],
                                     start=True, stop=True)
                    nc.tensor.matmul(PS[:, n % 3, N + 128:2 * N], k[:, N:odd], q[:, 128 * par:128 * par + 128],
                                     start=True, stop=True).then_inc(st_ready, 1)

            def values(V, chunk):
                b, g0 = V // 2, UP * (V % 2)
                if chunk == 0:
                    pe.wait_ge(exp_done, 2 * UP * (V + 1))
                    pe.wait_ge(vp_ready, b + 1)
                    if V >= 2:
                        pe.wait_ge(ot_done, V - 1)
                if chunk == 1:
                    pe.wait_ge(sel_done, UP * V + UP)
                for par in {0: (None,), 1: (0,), 2: (1,), 3: (0, 1)}[chunk]:
                    for j in range(UP):
                        w = pt[:, V % 2, j, :].rearrange("p (e c) -> p e c", e=2)
                        if chunk == 0:
                            blk, q0, w = g0 + j, 0, w[:, :, N + 128:2 * N]
                        elif chunk < 3:
                            blk, q0, w = PAIRS + 2 * (g0 + j) + par, 0, w[:, par, 0:N]
                        else:
                            blk, q0, w = 3 * PAIRS + 2 * (g0 + j) + par, 128, w[:, par, N:N + 128]
                        c = nc.tensor.matmul(O(V)[VW * j:VW * j + VW, q0:N], vp[:, b % 2, blk, :], w,
                                             start=(chunk == 0), stop=(chunk == 3 and par == 1))
                if chunk == 3:
                    c.then_inc(pv_done, 1)

            def maxima_t(U):
                pe.wait_ge(max_done, 3 * UP * (U + 1))
                if U >= 1:
                    pe.wait_ge(mlo_done, U)
                for t in range(2):
                    c = nc.tensor.transpose(MT[:, 128 * t:128 * t + 128],
                                            mx[:, U % 2, t, :, :].rearrange("p q g -> p (q g)"), ident[:, :])
                c.then_inc(mT_ready, 1)

            def denominators(V):
                pe.wait_ge(ot_done, V + 1)
                if V + 3 < UNITS:
                    pe.wait_ge(mlo_done, V + 4)
                nc.tensor.matmul(MISC, spread[:, :], ots[:, V % 2, :], start=True, stop=True).then_inc(den_ready, 1)

            def project(b):
                pe.wait_ge(att_done, 2 * b + 2)
                if b == 0:
                    pe.wait_ge(tanh_done, 1)
                for t in range(2):
                    for u in range(2):
                        c = nc.tensor.matmul(MISC[:, 128 * t:128 * t + 128], att[:, u, 128 * t:128 * t + 128],
                                             wos[:, u, :], start=(u == 0), stop=(u == 1))
                c.then_inc(y_ready, 1)

            def turn_tokens(b):
                pe.wait_ge(h2_ready, b + 1)
                if 2 * b + 3 <= UNITS:
                    pe.wait_ge(rec_done, 2 * b + 3)
                for t in range(2):
                    c = nc.tensor.transpose(MISC[:, 128 * t:128 * t + 128], rows[:, b % 2, 0, t, 0:D], ident[:, :])
                c.then_inc(h2T_ready, 1)

            def logits(b):
                pe.wait_ge(h2T_done, b + 1)
                for t in range(2):
                    c = nc.tensor.matmul(LOGITS[:, t, :], h2t[:, 128 * t:128 * t + 128], wgs[:, :],
                                         start=True, stop=True)
                c.then_inc(lg_ready, 1)

            def positions(b):
                pe.wait_ge(lab_ready, b + 1)
                pe.wait_ge(route, S_ROUTE * b)
                if b + 2 <= B:
                    pe.wait_ge(x1_done, b + 2)
                cur, rn = lab[:, b % 2, :, :], run[:, b % 2, :]
                nc.tensor.matmul(POS[:, 0, :], tri[:, :], cur[:, 0, :], start=True, stop=False)
                nc.tensor.matmul(POS[:, 0, :], ones[:, :], rn, start=False, stop=True)
                nc.tensor.matmul(POS[:, 1, :], tri[:, :], cur[:, 1, :], start=True, stop=False)
                nc.tensor.matmul(POS[:, 1, :], ones[:, :], cur[:, 0, :], start=False, stop=False)
                nc.tensor.matmul(POS[:, 1, :], ones[:, :], rn, start=False, stop=True).then_inc(pos_ready, 1)

            pe.wait_ge(consts, 15)
            pe.wait_ge(cast, 5)
            pe.wait_ge(q3_done, GROUPS)
            pe.wait_ge(k3_done, GROUPS + 1)
            pe.wait_ge(v_done, GROUPS + 1)
            for U in range(-2, UNITS + 6):
                for g in range(UP):
                    if 0 <= U < UNITS:
                        scores_t(U, g)
                    if U + 2 < UNITS:
                        scores(U + 2, g)
                    if g == 0 and -1 <= U and U + 1 < UNITS:
                        if U % 2 and 0 <= (U - 5) // 2:
                            pe.wait_ge(route, S_ROUTE * ((U - 5) // 2) + 1)
                        if U % 2 == 0 and 0 <= (U - 6) // 2:
                            pe.wait_ge(wts_done, S_WTS * ((U - 6) // 2) + 3)
                        if U == 4:
                            pe.wait_ge(x1_done, 1)
                        maxima_t(U + 1)
                    if 0 <= U - 1 < UNITS:
                        values(U - 1, g)
                    if g == 1 and 0 <= U - 2 < UNITS:
                        if U + 1 >= UNITS:
                            if U % 2:
                                pe.wait_ge(route, S_ROUTE * ((U - 5) // 2) + 1)
                            else:
                                pe.wait_ge(wts_done, S_WTS * ((U - 6) // 2) + 3)
                        denominators(U - 2)
                    if g == 2 and U % 2 and 0 <= (U - 3) // 2 < B:
                        project((U - 3) // 2)
                    if g == 2 and U % 2 == 0 and 0 <= (U - 4) // 2 < B:
                        if U - 2 >= UNITS:
                            pe.wait_ge(wts_done, S_WTS * ((U - 6) // 2) + 3)
                        turn_tokens((U - 4) // 2)
                    if g == 3 and U % 2 == 0 and 0 <= (U - 4) // 2 < B:
                        logits((U - 4) // 2)
                    if g == 3 and U % 2 and 0 <= (U - 5) // 2 < B:
                        positions((U - 5) // 2)

            def turn(e):
                pe.wait_ge(ex_in[e], 32)
                if e >= 2:
                    pe.wait_ge(xT_done, e - 1)
                for s in range(ST_TILES):
                    n = 128 if s < ST_TILES - 1 else LAST
                    c = nc.tensor.transpose(PS[:, e % 2, 128 * s:128 * s + n], ex[0:n, e, s, 0:D], ident[0:n, 0:n])
                c.then_inc(xT_ready, 1)

            def up(e):
                pe.wait_ge(wx_in[e % 2], 48 * (e // 2 + 1))
                pe.wait_ge(xT_done, e + 1)
                for c in range(HC):
                    n = HC * e + c
                    if n >= 2:
                        pe.wait_ge(hid_done, n - 1)
                    nc.tensor.matmul(PS[:, 2 + n % 2, 0:CAP], w1s[:, e % 2, 128 * c:128 * c + 128], xT[:, e % 2, :],
                                     start=True, stop=True)
                    nc.tensor.matmul(PS[:, 4 + n % 2, 0:CAP], w2s[:, e % 2, 128 * c:128 * c + 128], xT[:, e % 2, :],
                                     start=True, stop=True).then_inc(h_ready, 1)

            def down(e):
                pe.wait_ge(hid_done, HC * (e + 1))
                if e >= 2:
                    pe.wait_ge(yr_done, e - 1)
                for s in range(ST_TILES):
                    n = 128 if s < ST_TILES - 1 else LAST
                    for c in range(HC):
                        m = nc.tensor.matmul(PS[0:n, 6 + e % 2, 128 * s:128 * s + D],
                                             hid[:, e % 2, c, 128 * s:128 * s + n], w3s[:, e % 2, c, :],
                                             start=(c == 0), stop=(c == HC - 1))
                m.then_inc(yo_ready, 1)

            turn(0)
            for e in range(E):
                up(e)
                if e + 1 < E:
                    turn(e + 1)
                down(e)
        del block
    return nc


def x_tiles(ap):
    return ap.rearrange("b (t p) d -> p (b t) d", p=128)


def kernel(x, ctx_1024, g_xattn, g_ffn, L0_xattn_Wq, L0_xattn_Wkv, L0_xattn_Wout, L0_xattn_bout,
           L0_ffn_Wg, L0_ffn_bg, L0_ffn_W1, L0_ffn_W2, L0_ffn_W3):
    import numpy as _np
    import concourse.bacc as _bacc
    from concourse import mybir as _mybir
    from concourse.bass_utils import run_bass_kernel_spmd as _run

    def by_parity(w):
        return _np.asarray(w).reshape(128, 8, 2, 8).transpose(0, 2, 3, 1).reshape(128, 128)

    wkv = _np.asarray(L0_xattn_Wkv)
    ins = {"x": x, "ctx": ctx_1024, "g_xattn": g_xattn, "g_ffn": g_ffn, "wq": by_parity(L0_xattn_Wq),
           "wk": by_parity(wkv[:, :128]), "wv": wkv[:, 128:], "wout": L0_xattn_Wout, "bout": L0_xattn_bout,
           "wg": L0_ffn_Wg, "bg": L0_ffn_bg, "w1": L0_ffn_W1, "w2": L0_ffn_W2, "w3": L0_ffn_W3}
    nc = _bacc.Bacc("TRN2", target_bir_lowering=False, num_devices=1)
    arrays, args = {}, {}
    for name, a in ins.items():
        a = _np.ascontiguousarray(a)
        arrays[f"in_{name}"] = a
        args[name] = nc.dram_tensor(f"in_{name}", a.shape, _mybir.dt.from_np(a.dtype), kind="ExternalInput").ap()
    fp32 = _mybir.dt.float32
    args["slots_dram"] = nc.dram_tensor("slots", (8 * 320, 130), fp32, kind="Internal").ap()
    args["answers_dram"] = nc.dram_tensor("answers", (2 * 2048, 128), fp32, kind="Internal").ap()
    args["out"] = nc.dram_tensor("out_0", (8, 256, 128), fp32, kind="ExternalOutput").ap()
    flamingo_gated_block(nc, **args)
    r = _run(nc, [arrays], core_ids=[0])
    return r.results[0]["out_0"]
```

```python
import concourse.bass as bass
from concourse import mybir
from contextlib import ExitStack


def flamingo_gated_block(nc, x, ctx, g_xattn, g_ffn, wq, wk, wv, wout, bout, wg, bg, w1, w2, w3,
                         slots_dram, answers_dram, out):
    fp32, bf16 = mybir.dt.float32, mybir.dt.bfloat16
    i32, u32 = mybir.dt.int32, mybir.dt.uint32
    ALU = mybir.AluOpType
    ACT = mybir.ActivationFunctionType
    AX = mybir.AxisListType

    B, N, D = x.shape
    M = ctx.shape[1]
    HEADS, HD = 16, 8
    PAIRS = HEADS // 2
    UP = 4
    UNITS = 2 * B
    KEYS = M + N
    T = B * N
    TILES = T // 128
    GROUPS = TILES // 4
    E, _, H = w1.shape
    HC = H // 128
    TOPK = 2
    CAP = int(T / E * 1.25)
    SLOTS = E * CAP
    ST_TILES = (CAP + 127) // 128
    LAST = CAP - 128 * (ST_TILES - 1)
    SCALE = float(HD) ** -0.5
    RING = 3
    QROW = 6 * HD
    MROW = 2 * QROW
    KROWS = MROW + 4
    QPART = (0, 0, 0, 1, 1, 2)
    KPART = (0, 1, 2, 0, 1, 0)
    VW = 32
    ROW = D + 2
    NEVER = 1 << 22
    MASKED = -1e30
    EPS = 1e-5

    es = ExitStack()
    with es:
        def sb(name, shape, dt=fp32):
            return es.enter_context(nc.sbuf_tensor(name, shape, dt))

        def sem(name):
            return es.enter_context(nc.semaphore(name))

        PS = es.enter_context(nc.psum_tensor("PS", [128, 8, 512], fp32))

        xs = sb("xs", [128, TILES, D])
        kst = sb("kst", [128, RING, PAIRS, 2, 2 * KEYS], bf16)
        qst = sb("qst", [128, RING, PAIRS, 2, N], bf16)
        pt = sb("pt", [128, 2, UP, 1024])
        vraw = sb("vraw", [128, B, 3, D])
        vp = sb("vp", [128, 2, 5 * PAIRS, VW])
        kp = sb("kp", [128, GROUPS, 3, 2, KEYS + M], bf16)
        qp = sb("qp", [128, GROUPS, 3, 512], bf16)
        w1s = sb("w1s", [128, 2, H])
        w2s = sb("w2s", [128, 2, H])
        w3s = sb("w3s", [128, 2, HC, D])
        wqs = sb("wqs", [128, D])
        wks = sb("wks", [128, D])
        wvs = sb("wvs", [128, D])
        wos = sb("wos", [128, D])
        bos = sb("bos", [1, D])
        onesf = sb("onesf", [1, 128])
        wgs = sb("wgs", [128, E])
        bg2 = sb("bg2", [128, 2, E])
        gx = sb("gx", [128, 1])
        gf = sb("gf", [128, 1])
        tgx = sb("tgx", [128, 1])
        tgf = sb("tgf", [128, 1])
        ident = sb("ident", [128, 128])
        identb = sb("identb", [128, 128], bf16)
        maskb = sb("maskb", [128, 2, 128], bf16)
        tri = sb("tri", [128, 128], bf16)
        ones = sb("ones", [128, 128], bf16)
        half = sb("half", [128, 4])
        iotak = sb("iotak", [128, 4, E])
        dest_meta = sb("dest_meta", [128, TILES, 2], i32)
        blank = sb("blank", [128, ROW])
        stats = sb("stats", [128, 4, 6])
        mv = sb("mv", [128, 2, 4, 2])
        veps = sb("veps", [128, 2, 4])
        rstd = sb("rstd", [128, 2, 4])
        mx = sb("mx", [128, 2, 2, 2, UP])
        mxb = sb("mxb", [128, 2, 2, 2, 2 * UP], bf16)
        mrow = sb("mrow", [4 * UP, 2, N], bf16)
        ots = sb("ots", [128, 2, N])
        rec = sb("rec", [128, 2, UP, 2])
        att = sb("att", [128, 2, 2, D])
        attT = sb("attT", [128, N])
        h2t = sb("h2t", [128, N])
        rows = sb("rows", [128, 2, TOPK, 2, ROW])
        lg = sb("lg", [128, 2, E])
        top = sb("top", [128, 2, 8])
        topi = sb("topi", [128, 2, 8], u32)
        idxf = sb("idxf", [128, 4])
        oh = sb("oh", [128, 4, E])
        lab = sb("lab", [128, 2, 2, E], bf16)
        run = sb("run", [128, 2, E], bf16)
        run1 = sb("run1", [128, E], bf16)
        d01 = sb("d01", [128, 2])
        e01 = sb("e01", [128, 2])
        s01 = sb("s01", [128, 2])
        ohp = sb("ohp", [128, 4, E])
        posk = sb("posk", [128, 4])
        over = sb("over", [128, 4])
        slotf = sb("slotf", [128, 4])
        dest = sb("dest", [128, 2, 4], u32)

        ptf = pt[:, :, :, :].rearrange("p a b c -> p (a b c)")
        zeros = ptf[:, 0:1024]
        xn = [ptf[:, 1024 + 512 * i:1536 + 512 * i].rearrange("p (t d) -> p t d", d=D) for i in range(2)]
        hT = [ptf[:, 2048 + 512 * i:2560 + 512 * i] for i in range(2)]
        ctxT = ptf[:, 3072:4096].rearrange("p (b c) -> p b c", c=128)
        ctxs = ptf[:, 4096:4608].rearrange("p (t d) -> p t d", d=D)
        rq = [ptf[:, 4608 + 512 * i:5120 + 512 * i] for i in range(2)]
        rk = [ptf[:, 5632 + 512 * i:6144 + 512 * i] for i in range(2)]

        zrow = ptf[0:QROW, 6656:6656 + KEYS // 2].bitcast(bf16)
        frow = ptf[0:4, 6656 + KEYS // 2:6656 + 3 * KEYS // 2].bitcast(bf16).rearrange("p (a k) -> p a k", a=2)

        kf = kst[:, :, :, :, :].rearrange("p a b c d -> p (a b c d)").bitcast(fp32)
        o = 0

        def room(n):
            nonlocal o
            o += n
            return kf[:, o - n:o]

        ex = room(E * ST_TILES * ROW).rearrange("p (e s c) -> p e s c", e=E, s=ST_TILES)
        xT = room(2 * CAP).rearrange("p (a c) -> p a c", a=2)
        gate = room(2 * CAP).rearrange("p (a c) -> p a c", a=2)
        hid = room(2 * HC * CAP).rearrange("p (a h c) -> p a h c", a=2, h=HC)
        yr = room(2 * ST_TILES * D).rearrange("p (a s d) -> p a s d", a=2, s=ST_TILES)
        qf = qst[:, :, :, :, :].rearrange("p a b c d -> p (a b c d)").bitcast(fp32)
        yy = qf[:, 0:TOPK * TILES * D].rearrange("p (k t d) -> p k t d", k=TOPK, t=TILES)

        w_in = sem("w_in")
        x_in = [sem(f"x_in{g}") for g in range(GROUPS)]
        ctx_in = sem("ctx_in")
        small_in = sem("small_in")
        zeroed = sem("zeroed")
        fixed_in = [sem(f"fixed_in{s}") for s in range(RING)]
        consts = sem("consts")
        cast = sem("cast")
        dram_zero = sem("dram_zero")
        stat = sem("stat")
        eps_added = sem("eps_added")
        rstd_ready = sem("rstd_ready")
        xn_ready = sem("xn_ready")
        tr_ready = sem("tr_ready")
        hT_ready = sem("hT_ready")
        q_ready = sem("q_ready")
        k_ready = sem("k_ready")
        v_ready = sem("v_ready")
        q1_done = sem("q1_done")
        k1_done = sem("k1_done")
        rq_done = sem("rq_done")
        rk_done = sem("rk_done")
        q2_done = sem("q2_done")
        k2_done = sem("k2_done")
        q3_done = sem("q3_done")
        k3_done = sem("k3_done")
        ctx_done = sem("ctx_done")
        v_done = sem("v_done")
        stack_in = [sem(f"stack_in{g}") for g in range(GROUPS)]
        s_ready = sem("s_ready")
        max_done = sem("max_done")
        split_done = sem("split_done")
        mT_ready = sem("mT_ready")
        mrow_done = sem("mrow_done")
        m_in = [sem(f"m_in{i}") for i in range(2)]
        st_ready = sem("st_ready")
        exp_done = sem("exp_done")
        sel_done = sem("sel_done")
        vp_ready = sem("vp_ready")
        pv_done = sem("pv_done")
        ot_done = sem("ot_done")
        oT_ready = sem("oT_ready")
        rec_done = sem("rec_done")
        att_done = sem("att_done")
        attT_ready = sem("attT_ready")
        attT_done = sem("attT_done")
        y_ready = sem("y_ready")
        x1_done = sem("x1_done")
        tanh_done = sem("tanh_done")
        h2_ready = sem("h2_ready")
        h2T_ready = sem("h2T_ready")
        h2T_done = sem("h2T_done")
        row1_done = sem("row1_done")
        lg_ready = sem("lg_ready")
        route = sem("route")
        lab_ready = sem("lab_ready")
        d01_ready = sem("d01_ready")
        e01_done = sem("e01_done")
        pos_ready = sem("pos_ready")
        wts_done = sem("wts_done")
        dest_ready = sem("dest_ready")
        sent = [sem(f"sent{i}") for i in range(2)]
        wx_in = [sem(f"wx_in{i}") for i in range(2)]
        ex_in = [sem(f"ex_in{e}") for e in range(E)]
        xT_ready = sem("xT_ready")
        xT_done = sem("xT_done")
        h_ready = sem("h_ready")
        gate_done = sem("gate_done")
        hid_done = sem("hid_done")
        yo_ready = sem("yo_ready")
        yr_done = sem("yr_done")
        answered = [sem(f"answered{i}") for i in range(2)]
        yy_in = [sem(f"yy_in{g}") for g in range(GROUPS)]
        sum_done = sem("sum_done")
        out_done = sem("out_done")
        stored = sem("stored")

        S_ROUTE = 7
        S_WTS = 5
        S_STAT = 8
        MT = PS[0:4 * UP, 7, N:2 * N]
        OT = PS[:, 7, 0:N].rearrange("p (t j c) -> p t j c", t=2, j=UP)
        MISC = PS[:, 3, 0:N]
        LOGITS = PS[:, 3, 0:2 * E].rearrange("p (t e) -> p t e", e=E)
        POS = PS[:, 3, 2 * E:4 * E].rearrange("p (t e) -> p t e", e=E)
        O = PS[:, 6, 0:N]

        def place(U):
            b = U // 2
            return (b // 2) % RING, b % 2, UP * (U % 2)

        block = es.enter_context(nc.Block())

        @block.sync
        def _(sp):
            sp.dma_start(xs[:, 0:4, :], x_tiles(x)[:, 0:4, :]).then_inc(x_in[0], 16)
            for w, s in ((wq, wqs), (wk, wks), (wv, wvs)):
                sp.dma_start(s[:, :], w).then_inc(w_in, 16)
            for g in range(1, GROUPS):
                sp.dma_start(xs[:, 4 * g:4 * g + 4, :], x_tiles(x)[:, 4 * g:4 * g + 4, :]).then_inc(x_in[g], 16)

            def load_stack(g, quarters=range(4)):
                s = g % RING
                for quarter in quarters:
                    par = quarter % 2
                    for r in range(6):
                        row = QROW * par + HD * r
                        if quarter < 2:
                            sp.wait_ge(q3_done, g + 1)
                            sp.dma_start(qst[row:row + HD, s, :, :, :].rearrange("p g b n -> p g (b n)"),
                                         qp[64 * par:64 * par + 64, g, QPART[r], :]).then_inc(stack_in[g], 16)
                        else:
                            sp.wait_ge(ctx_done, 1)
                            sp.wait_ge(k3_done, g + 1)
                            sp.dma_start(kst[row:row + HD, s, :, :, KEYS * par:KEYS * (par + 1)],
                                         kp[64 * par:64 * par + 64, g, KPART[r], :, M * (1 - par):M * (1 - par) + KEYS]
                                         ).then_inc(stack_in[g], 16)

            def load_maxima(U):
                s, bb, g0 = place(U)
                sp.wait_ge(mrow_done, U + 1)
                for par in range(2):
                    for part in range(2):
                        row = MROW + 2 * par + part
                        sp.dma_start(qst[row:row + 1, s, g0:g0 + UP, bb, :],
                                     mrow[UP * (2 * part + par):UP * (2 * part + par + 1), U % 2, :]).then_inc(m_in[U % 2], 16)

            def load_expert(e):
                if e >= 2:
                    sp.wait_ge(yo_ready, e - 1)
                sp.dma_start(w1s[:, e % 2, :], w1[e]).then_inc(wx_in[e % 2], 16)
                sp.dma_start(w2s[:, e % 2, :], w2[e]).then_inc(wx_in[e % 2], 16)
                sp.dma_start(w3s[:, e % 2, :, :], w3[e].rearrange("(c p) d -> p c d", p=128)
                             ).then_inc(wx_in[e % 2], 16)

            sp.wait_ge(zeroed, 1)
            for s in range(RING):
                for rows_, k0, src in ((slice(0, QROW), KEYS, zrow), (slice(QROW, MROW), 0, zrow)):
                    sp.dma_start(kst[rows_, s, :, :, k0:k0 + KEYS].rearrange("p g b k -> p (g b) k"),
                                 bass.AP(tensor=src.tensor, offset=src.offset,
                                         ap=[src.ap[0], [0, 2 * PAIRS], [1, KEYS]])).then_inc(fixed_in[s], 16)
                src = frow[:, :, :]
                sp.dma_start(kst[MROW:KROWS, s, :, :, :].rearrange("p g b k -> p (g b) k"),
                             bass.AP(tensor=src.tensor, offset=src.offset,
                                     ap=[src.ap[0], [0, 2 * PAIRS], [1, 2 * KEYS]])).then_inc(fixed_in[s], 16)
            load_stack(0)
            load_stack(1)
            for U in range(UNITS):
                load_maxima(U)
                if U < 4:
                    load_stack(2, (U,))
                elif U < 8:
                    if U == 4:
                        sp.wait_ge(st_ready, 4 * 2 * UP)
                    load_stack(RING, (U - 4,))
                if U == 8:
                    load_expert(0)
                    load_expert(1)
            for i in range(2):
                sp.wait_ge(sent[i], 16 * 4 * B // 2)
            sp.wait_ge(st_ready, 2 * UP * UNITS)
            for e in range(E):
                r0 = e * CAP
                sp.dma_start(ex[:, e, 0:ST_TILES - 1, :],
                             slots_dram[r0:r0 + 128 * (ST_TILES - 1), :].rearrange("(s p) c -> p s c", p=128)
                             ).then_inc(ex_in[e], 16)
                sp.dma_start(ex[0:LAST, e, ST_TILES - 1, :],
                             slots_dram[r0 + 128 * (ST_TILES - 1):r0 + CAP, :]).then_inc(ex_in[e], 16)
            for e in range(2, E):
                load_expert(e)
            for i in range(2):
                sp.wait_ge(answered[i], 16 * ST_TILES * E // 2)
            av = answers_dram.rearrange("(k t p) d -> k p t d", k=TOPK, p=128)
            for g in range(GROUPS):
                for k in range(TOPK):
                    sp.dma_start(yy[:, k, 4 * g:4 * g + 4, :], av[k, :, 4 * g:4 * g + 4, :]).then_inc(yy_in[g], 16)
            for g in range(GROUPS):
                sp.wait_ge(out_done, g + 1)
                sp.dma_start(x_tiles(out)[:, 4 * g:4 * g + 4, :], xs[:, 4 * g:4 * g + 4, :]).then_inc(stored, 16)
            sp.wait_ge(stored, 16 * GROUPS)

        @block.gpsimd
        def _(pool):
            nc.gpsimd.memset(ident[:, :], 0.0).then_inc(consts, 1)
            pool.wait_ge(consts, 1)
            nc.gpsimd.affine_select(out=ident[:, :], in_=ident[:, :], compare_op=ALU.not_equal, fill=1.0, base=0,
                                    pattern=[[-1, 128]], channel_multiplier=1).then_inc(consts, 1)
            nc.gpsimd.memset(half[:, :], -0.5).then_inc(consts, 1)
            nc.gpsimd.memset(maskb[:, :, :], 0.0).then_inc(consts, 1)
            nc.gpsimd.memset(onesf[:, :], 1.0).then_inc(consts, 1)
            nc.gpsimd.memset(ones[:, :], 1.0).then_inc(consts, 1)
            nc.gpsimd.memset(zeros, 0.0).then_inc(consts, 1)
            nc.gpsimd.memset(blank[:, :], 0.0).then_inc(consts, 1)
            pool.wait_ge(consts, 8)
            nc.gpsimd.affine_select(out=maskb[:, :, :], in_=maskb[:, :, :], compare_op=ALU.is_ge, fill=MASKED, base=0,
                                    pattern=[[0, 2], [-1, 128]], channel_multiplier=1).then_inc(consts, 1)
            nc.gpsimd.affine_select(out=tri[:, :], in_=ones[:, :], compare_op=ALU.is_ge, fill=0.0, base=0,
                                    pattern=[[1, 128]], channel_multiplier=-1).then_inc(consts, 1)
            nc.gpsimd.iota(iotak[:, :, :], pattern=[[0, 4], [1, E]], base=0, channel_multiplier=0,
                           allow_small_or_imprecise_dtypes=True).then_inc(consts, 1)
            nc.gpsimd.iota(dest_meta[:, :, :], pattern=[[128, TILES], [T, 2]], base=0,
                           channel_multiplier=1).then_inc(consts, 1)
            nc.gpsimd.iota(blank[:, D:D + 1].bitcast(i32), pattern=[[0, 1]], base=NEVER,
                           channel_multiplier=0).then_inc(consts, 1)

            pool.wait_ge(consts, 13)
            av = answers_dram.rearrange("(z p n) d -> z p (n d)", z=4, p=128)
            for z in range(4):
                nc.gpsimd.dma_start(av[z], zeros).then_inc(dram_zero, 16)
            bv = blank[:, :]
            nc.gpsimd.dma_start(slots_dram.rearrange("(n p) c -> p n c", p=128),
                                bass.AP(tensor=bv.tensor, offset=bv.offset,
                                        ap=[bv.ap[0], [0, SLOTS // 128], [1, ROW]])).then_inc(dram_zero, 16)

            def rstd_of(n, par, count, stats_by):
                pool.wait_ge(stat, stats_by)
                nc.gpsimd.tensor_scalar(veps[:, par, 0:count], mv[:, par, 0:count, 1], 1.0, EPS, ALU.mult,
                                        ALU.add).then_inc(eps_added, 1)
                pool.wait_ge(eps_added, n + 1)
                nc.gpsimd.tensor_tensor(rstd[:, par, 0:count], veps[:, par, 0:count], half[:, 0:count],
                                        ALU.pow).then_inc(rstd_ready, 1)

            def third_parts(g):
                i = (g + 1) % 2
                pool.wait_ge(q2_done, g + 1)
                nc.gpsimd.tensor_tensor(qp[:, g, 2, :], rq[g % 2], qp[:, g, 1, :], ALU.subtract
                                        ).then_inc(q3_done, 1)
                pool.wait_ge(k2_done, g + 2)
                nc.gpsimd.tensor_tensor(kp[:, g, 2, :, M:KEYS], rk[i].rearrange("p (b n) -> p b n", b=2),
                                        kp[:, g, 1, :, M:KEYS], ALU.subtract).then_inc(k3_done, 1)

            def norm_batch(b):
                rstd_of(GROUPS + b, b % 2, 2, S_STAT * GROUPS + 4 * (b + 1))

            rstd_of(0, 0, 4, S_STAT)
            for g in range(GROUPS):
                if g + 1 < GROUPS:
                    rstd_of(g + 1, (g + 1) % 2, 4, S_STAT * (g + 2))
                third_parts(g)
            for U in range(UNITS + 4):
                if U < UNITS:
                    for g in range(UP):
                        pool.wait_ge(exp_done, 2 * (UP * U + g + 1))
                        v = pt[:, U % 2, g, :].rearrange("p (s c) -> p s c", s=4)[:, :, 0:128]
                        nc.gpsimd.affine_select(out=v, in_=v, compare_op=ALU.is_ge, fill=0.0, base=0,
                                                pattern=[[0, 4], [1, 128]],
                                                channel_multiplier=-1).then_inc(sel_done, 1)
                        if g == 0 and U % 2 == 0 and 0 <= (U - 4) // 2 < B:
                            norm_batch((U - 4) // 2)
                elif U % 2 == 0 and 0 <= (U - 4) // 2 < B:
                    norm_batch((U - 4) // 2)
                if U % 2 and 0 <= (U - 5) // 2 < B:
                    b = (U - 5) // 2
                    if b == 0:
                        pool.wait_ge(dram_zero, 16 * 5)
                    pool.wait_ge(dest_ready, b + 1)
                    pool.wait_ge(row1_done, b + 1)
                    for k in range(TOPK):
                        for t in range(2):
                            nc.gpsimd.indirect_dma_start(
                                out=slots_dram, out_offset=bass.IndirectOffsetOnAxis(
                                    ap=dest[:, b % 2, 2 * t + k:2 * t + k + 1], axis=0),
                                in_=rows[:, b % 2, k, t, :], in_offset=None,
                                bounds_check=SLOTS - 1, oob_is_err=False).then_inc(sent[b % 2], 16)
            for e in range(E):
                pool.wait_ge(yr_done, e + 1)
                for s in range(ST_TILES):
                    n = 128 if s < ST_TILES - 1 else LAST
                    nc.gpsimd.indirect_dma_start(
                        out=answers_dram, out_offset=bass.IndirectOffsetOnAxis(
                            ap=ex[0:n, e, s, D:D + 1].bitcast(u32), axis=0),
                        in_=yr[0:n, e % 2, s, :], in_offset=None,
                        bounds_check=TOPK * T - 1, oob_is_err=False).then_inc(answered[e % 2], 16)

        @block.scalar
        def _(act):
            act.dma_start(ctxs, ctx.rearrange("b m d -> (b m) d").rearrange("(t p) d -> p t d", p=128)
                          ).then_inc(ctx_in, 16)
            act.dma_start(gx[:, :], g_xattn.partition_broadcast(128)).then_inc(small_in, 16)
            act.dma_start(gf[:, :], g_ffn.partition_broadcast(128)).then_inc(small_in, 16)
            act.dma_start(wgs[:, :], wg).then_inc(small_in, 16)
            for t in range(2):
                act.dma_start(bg2[:, t, :], bg.partition_broadcast(128)).then_inc(small_in, 16)
            act.dma_start(wos[:, :], wout).then_inc(small_in, 16)
            act.dma_start(bos[:, :], bout.rearrange("(a n) -> a n", a=1)).then_inc(small_in, 16)

            act.wait_ge(tr_ready, 1)
            v = PS[:, 0, :].rearrange("p (b m) -> p b m", m=M)
            nc.scalar.copy(ctxT[:, :, 0:M], v)
            nc.scalar.copy(ctxT[:, :, M:2 * M], v).then_inc(hT_ready, 1)
            act.wait_ge(k_ready, 1)
            kc = PS[:, 4, :].rearrange("p (g b m) -> p g b m", g=GROUPS, b=2)
            nc.scalar.copy(kp[:, :, 0, :, 0:M], kc).then_inc(k1_done, 1)
            act.wait_ge(v_ready, 1)
            nc.scalar.copy(vraw[:, 0:4, 0, :], PS[:, 6, :].rearrange("p (b d) -> p b d", d=D))
            nc.scalar.copy(vraw[:, 4:8, 0, :], PS[:, 2, :].rearrange("p (b d) -> p b d", d=D)).then_inc(v_done, 1)
            act.wait_ge(rk_done, 1)
            nc.scalar.copy(kp[:, :, 1, :, 0:M], rk[0].rearrange("p (g b m) -> p g b m", g=GROUPS, b=2)
                           ).then_inc(k2_done, 1)
            for g in range(GROUPS):
                i = (g + 1) % 2
                act.wait_ge(tr_ready, g + 2)
                if g >= 2:
                    act.wait_ge(v_ready, g)
                nc.scalar.copy(hT[g % 2], PS[:, i, :]).then_inc(hT_ready, 1)
                act.wait_ge(q_ready, g + 1)
                nc.scalar.copy(qp[:, g, 0, :], PS[:, 2 + i, :]).then_inc(q1_done, 1)
                act.wait_ge(k_ready, g + 2)
                nc.scalar.copy(kp[:, g, 0, :, M:KEYS], PS[:, 4 + i, :].rearrange("p (b n) -> p b n", b=2)
                               ).then_inc(k1_done, 1)
                act.wait_ge(v_ready, g + 2)
                nc.scalar.copy(vraw[:, 2 * g:2 * g + 2, 1:3, :],
                               PS[:, 6 + i, :].rearrange("p (b t d) -> p b t d", b=2, t=2)).then_inc(v_done, 1)
                act.wait_ge(rq_done, g + 1)
                nc.scalar.copy(qp[:, g, 1, :], rq[g % 2]).then_inc(q2_done, 1)
                act.wait_ge(rk_done, g + 2)
                nc.scalar.copy(kp[:, g, 1, :, M:KEYS], rk[i].rearrange("p (b n) -> p b n", b=2)
                               ).then_inc(k2_done, 1)
            act.wait_ge(small_in, 16 * 7)
            nc.scalar.activation(tgx[:, :], gx[:, :], ACT.Tanh)
            nc.scalar.activation(tgf[:, :], gf[:, :], ACT.Tanh).then_inc(tanh_done, 1)

            def maxima_row(U):
                act.wait_ge(mT_ready, U + 1)
                if U >= 2:
                    act.wait_ge(m_in[U % 2], 64 * (U // 2))
                nc.scalar.copy(mrow[:, U % 2, :], MT).then_inc(mrow_done, 1)

            def pad_values(b):
                if b == 0:
                    act.wait_ge(v_done, GROUPS + 1)
                if b >= 2:
                    act.wait_ge(pv_done, 2 * b - 2)
                for par in range(2):
                    lo = vraw[64 * par:64 * par + 64, b, 0, :].rearrange("p (g q d) -> p g q d", q=2, d=HD)
                    c0 = 9 * par
                    nc.scalar.copy(vp[64 * par:64 * par + 64, b % 2, 0:PAIRS, c0:c0 + HD], lo[:, :, par, :])
                    for blk in range(2):
                        dst = vp[:, b % 2, PAIRS * (1 + 2 * blk):PAIRS * (3 + 2 * blk), :].rearrange(
                            "p (g q) c -> p g q c", q=2)
                        src = vraw[:, b, 1 + blk, :].rearrange("p (g q d) -> p g q d", q=2, d=HD)
                        ins = nc.scalar.copy(dst[:, :, par, c0:c0 + HD], src[:, :, par, :])
                ins.then_inc(vp_ready, 1)

            maxima_row(0)
            for U in range(UNITS + 4):
                if U >= 2 and U - 2 < UNITS:
                    V = U - 2
                    act.wait_ge(pv_done, V + 1)
                    if V >= 2:
                        act.wait_ge(oT_ready, V - 1)
                    nc.scalar.copy(ots[:, V % 2, :], O).then_inc(ot_done, 1)
                for g in range(UP):
                    if U < UNITS:
                        if U == 0 and g == 0:
                            act.wait_ge(dram_zero, 16 * 5)
                            act.wait_ge(q3_done, GROUPS)
                            act.wait_ge(k3_done, GROUPS)
                            act.wait_ge(ctx_done, 1)
                            act.wait_ge(v_ready, GROUPS + 1)
                            for s in range(RING):
                                act.wait_ge(fixed_in[s], 16 * 3)
                        if U >= 2 and g == 0:
                            act.wait_ge(pv_done, U - 1)
                        for par in range(2):
                            n = 2 * (UP * U + g) + par
                            act.wait_ge(st_ready, n + 1)
                            nc.scalar.activation(pt[:, U % 2, g, 512 * par:512 * par + 512], PS[:, n % 3, :],
                                                 ACT.Exp, scale=SCALE).then_inc(exp_done, 1)
                    if g == 0 and U + 1 < UNITS:
                        maxima_row(U + 1)
                    if g == 1 and U % 2 == 0 and U // 2 < B:
                        pad_values(U // 2)
                    if g == 2 and U % 2 and 0 <= (U - 3) // 2 < B:
                        b = (U - 3) // 2
                        act.wait_ge(attT_ready, b + 1)
                        if b >= 1:
                            act.wait_ge(y_ready, b)
                        nc.scalar.copy(attT[:, :], MISC).then_inc(attT_done, 1)
                    if g == 2 and U % 2 == 0 and 0 <= (U - 4) // 2 < B:
                        b = (U - 4) // 2
                        act.wait_ge(h2T_ready, b + 1)
                        nc.scalar.copy(h2t[:, :], MISC).then_inc(h2T_done, 1)
                        if b >= 2:
                            act.wait_ge(sent[b % 2], 16 * 4 * (b // 2))
                        nc.scalar.copy(rows[:, b % 2, 1, :, 0:D], rows[:, b % 2, 0, :, 0:D]).then_inc(row1_done, 1)
                    if g == 0 and U % 2 and 0 <= (U - 5) // 2 < B:
                        b = (U - 5) // 2
                        act.wait_ge(d01_ready, b + 1)
                        nc.scalar.activation(e01[:, :], d01[:, :], ACT.Exp).then_inc(e01_done, 1)

            def tokens_in(e):
                act.wait_ge(xT_ready, e + 1)
                if e >= 2:
                    act.wait_ge(h_ready, HC * (e - 1))
                nc.scalar.copy(xT[:, e % 2, :], PS[:, e % 2, 0:CAP]).then_inc(xT_done, 1)

            tokens_in(0)
            for e in range(E):
                for c in range(HC):
                    n = HC * e + c
                    act.wait_ge(h_ready, n + 1)
                    if n >= 2:
                        act.wait_ge(hid_done, n - 1)
                    nc.scalar.activation(gate[:, n % 2, :], PS[:, 2 + n % 2, 0:CAP], ACT.Silu).then_inc(gate_done, 1)
                if e + 1 < E:
                    tokens_in(e + 1)

        @block.vector
        def _(dve):
            nc.vector.memset(zrow, 0.0)
            nc.vector.memset(frow[:, 0, :], 0.0)
            nc.vector.memset(frow[:, 1, :], -1.0).then_inc(cast, 1)
            dve.wait_ge(cast, 1)
            nc.vector.memset(frow[0:2, 0, :], -1.0)
            nc.vector.memset(frow[0:2, 1, :], 0.0).then_inc(zeroed, 1)

            def norm_tokens(g):
                dve.wait_ge(rstd_ready, g + 1)
                if g >= 2:
                    dve.wait_ge(tr_ready, g)
                for i in range(4):
                    c = nc.vector.tensor_scalar(xn[g % 2][:, i, :], xs[:, 4 * g + i, :], mv[:, g % 2, i, 0:1],
                                                rstd[:, g % 2, i:i + 1], ALU.subtract, ALU.mult)
                c.then_inc(xn_ready, 1)

            def ctx_parts():
                dve.wait_ge(k1_done, 1)
                kc = PS[:, 4, :].rearrange("p (g b m) -> p g b m", g=GROUPS, b=2)
                rv = rk[0].rearrange("p (g b m) -> p g b m", g=GROUPS, b=2)
                nc.vector.tensor_tensor(rv, kc, kp[:, :, 0, :, 0:M], ALU.subtract).then_inc(rk_done, 1)
                dve.wait_ge(k2_done, 1)
                nc.vector.tensor_tensor(kp[:, :, 2, :, 0:M], rv, kp[:, :, 1, :, 0:M], ALU.subtract
                                        ).then_inc(cast, 1)
                dve.wait_ge(cast, 3)
                allp = kp[:, :, :, :, :].rearrange("p g c b k -> p (g c b) k")
                nc.vector.tensor_copy(allp[:, :, KEYS:KEYS + M], allp[:, :, 0:M]).then_inc(ctx_done, 1)

            def parts(g):
                i = (g + 1) % 2
                dve.wait_ge(q1_done, g + 1)
                if g >= 2:
                    dve.wait_ge(q3_done, g - 1)
                nc.vector.tensor_tensor(rq[g % 2], PS[:, 2 + i, :], qp[:, g, 0, :], ALU.subtract
                                        ).then_inc(rq_done, 1)
                dve.wait_ge(k1_done, g + 2)
                if g >= 2:
                    dve.wait_ge(k3_done, g - 1)
                nc.vector.tensor_tensor(rk[i].rearrange("p (b n) -> p b n", b=2),
                                        PS[:, 4 + i, :].rearrange("p (b n) -> p b n", b=2),
                                        kp[:, g, 0, :, M:KEYS], ALU.subtract).then_inc(rk_done, 1)

            def stats_group(g):
                dve.wait_ge(x_in[g], 16)
                if g >= 1:
                    dve.wait_ge(stat, S_STAT * g)
                for i in range(4):
                    nc.vector.bn_stats(stats[:, i, :], xs[:, 4 * g + i, :]).then_inc(stat, 1)
                for i in range(4):
                    dve.wait_ge(stat, S_STAT * g + i + 1)
                    nc.vector.bn_aggr(mv[:, g % 2, i, :], stats[:, i, :]).then_inc(stat, 1)

            stats_group(0)
            norm_tokens(0)
            nc.vector.memset(vp[:, :, :, :].rearrange("p a b c -> p (a b c)"), 0.0).then_inc(cast, 1)
            dve.wait_ge(cast, 2)
            nc.vector.memset(vp[0:64, :, 0:PAIRS, 8:9], 1.0)
            nc.vector.memset(vp[64:128, :, 0:PAIRS, 17:18], 1.0)
            for par in range(2):
                v = vp[:, :, PAIRS:5 * PAIRS, :].rearrange("p a (g q) c -> p a g q c", q=2)
                nc.vector.memset(v[:, :, :, par, 8 + 9 * par:9 + 9 * par], 1.0)
            ctx_parts()
            for g in range(GROUPS):
                if g + 1 < GROUPS:
                    stats_group(g + 1)
                    norm_tokens(g + 1)
                parts(g)
            dve.wait_ge(consts, 13)
            nc.vector.tensor_copy(identb[:, :], ident[:, :])
            nc.vector.memset(run[:, 0, :], 0.0).then_inc(cast, 1)

            def maxima(U, g):
                n = 3 * (UP * U + g)
                dve.wait_ge(s_ready, n + 1)
                nc.vector.tensor_reduce(mx[:, U % 2, 0, :, g],
                                        PS[:, 4 + n % 2, 0:2 * (M + 128)].rearrange("p (q k) -> p q k", q=2),
                                        axis=AX.X, op=ALU.max).then_inc(max_done, 1)
                for par in range(2):
                    n += 1
                    dve.wait_ge(s_ready, n + 1)
                    nc.vector.tensor_reduce(mx[:, U % 2, 1, par, g:g + 1], PS[:, 4 + n % 2, 0:KEYS],
                                            axis=AX.X, op=ALU.max).then_inc(max_done, 1)

            def split_maxima(U):
                dve.wait_ge(max_done, 3 * UP * (U + 1))
                if U >= 2:
                    dve.wait_ge(mT_ready, U - 1)
                m = mx[:, U % 2, :, :, :].rearrange("p t q g -> p t (q g)")
                nc.vector.tensor_copy(mxb[:, U % 2, :, 0, :], m).then_inc(split_done, 1)
                dve.wait_ge(split_done, 2 * U + 1)
                nc.vector.tensor_tensor(mxb[:, U % 2, :, 1, :], m, mxb[:, U % 2, :, 0, :], ALU.subtract
                                        ).then_inc(split_done, 1)

            def normalize(V):
                b, g0 = V // 2, UP * (V % 2)
                dve.wait_ge(oT_ready, V + 1)
                nc.vector.reciprocal(rec[:, :, :, :], OT[:, :, :, HD:2 * HD + 2:HD + 1]).then_inc(rec_done, 1)
                dve.wait_ge(rec_done, V + 1)
                if b >= 2 and V % 2 == 0:
                    dve.wait_ge(attT_ready, b - 1)
                for t in range(2):
                    rv = rec[:, t, :, :]
                    c = nc.vector.tensor_tensor(
                        att[:, b % 2, t, 2 * HD * g0:2 * HD * (g0 + UP)].rearrange("p (j q d) -> p j q d", q=2, d=HD),
                        OT[:, t, :, 0:2 * HD + 2].rearrange("p j (q d) -> p j q d", q=2)[:, :, :, 0:HD],
                        bass.AP(tensor=rv.tensor, offset=rv.offset, ap=[rv.ap[0], [2, UP], [1, 2], [0, HD]]),
                        ALU.mult)
                c.then_inc(att_done, 1)

            def tokens_norm(b):
                base = S_STAT * GROUPS + 4 * b
                dve.wait_ge(y_ready, b + 1)
                if b == 0:
                    dve.wait_ge(tanh_done, 1)
                v = xs[:, 2 * b:2 * b + 2, :]
                nc.vector.scalar_tensor_tensor(v, MISC.rearrange("p (t d) -> p t d", t=2), tgx[:, 0:1], v,
                                               ALU.mult, ALU.add).then_inc(x1_done, 1)
                dve.wait_ge(x1_done, b + 1)
                dve.wait_ge(stat, base)
                for i in range(2):
                    nc.vector.bn_stats(stats[:, i, :], xs[:, 2 * b + i, :]).then_inc(stat, 1)
                for i in range(2):
                    dve.wait_ge(stat, base + i + 1)
                    nc.vector.bn_aggr(mv[:, b % 2, i, :], stats[:, i, :]).then_inc(stat, 1)

            def tokens_out(b):
                dve.wait_ge(rstd_ready, GROUPS + b + 1)
                if b >= 2:
                    dve.wait_ge(sent[b % 2], 16 * 4 * (b // 2))
                    dve.wait_ge(row1_done, b - 1)
                for i in range(2):
                    c = nc.vector.tensor_scalar(rows[:, b % 2, 0, i, 0:D], xs[:, 2 * b + i, :], mv[:, b % 2, i, 0:1],
                                                rstd[:, b % 2, i:i + 1], ALU.subtract, ALU.mult)
                c.then_inc(h2_ready, 1)

            def top_two(b):
                r = S_ROUTE * b
                dve.wait_ge(lg_ready, b + 1)
                nc.vector.tensor_tensor(lg[:, :, :], LOGITS, bg2[:, :, :], ALU.add).then_inc(route, 1)
                dve.wait_ge(route, r + 1)
                for t in range(2):
                    c = nc.vector.max(top[:, t, :], lg[:, t, :])
                c.then_inc(route, 1)
                dve.wait_ge(route, r + 2)
                for t in range(2):
                    c = nc.vector.max_index(topi[:, t, :], top[:, t, :], lg[:, t, :])
                c.then_inc(route, 1)
                nc.vector.tensor_tensor(d01[:, :], top[:, :, 1], top[:, :, 0], ALU.subtract).then_inc(d01_ready, 1)
                dve.wait_ge(route, r + 3)
                if b >= 1:
                    dve.wait_ge(dest_ready, b)
                nc.vector.tensor_copy(idxf[:, :].rearrange("p (t k) -> p t k", t=2), topi[:, :, 0:TOPK]
                                      ).then_inc(route, 1)
                dve.wait_ge(route, r + 4)
                iv = idxf[:, :]
                nc.vector.tensor_tensor(oh[:, :, :], iotak[:, :, :],
                                        bass.AP(tensor=iv.tensor, offset=iv.offset, ap=[iv.ap[0], [1, 4], [0, E]]),
                                        ALU.is_equal).then_inc(route, 1)
                dve.wait_ge(route, r + 5)
                ov = oh[:, :, :].rearrange("p (t k) e -> p t k e", k=TOPK)
                if b >= 2:
                    dve.wait_ge(pos_ready, b - 1)
                nc.vector.tensor_tensor(lab[:, b % 2, :, :], ov[:, :, 0, :], ov[:, :, 1, :], ALU.add
                                        ).then_inc(lab_ready, 1)
                dve.wait_ge(lab_ready, b + 1)
                nc.vector.tensor_tensor(run1[:, :], run[:, b % 2, :], lab[:, b % 2, 0, :], ALU.add).then_inc(route, 1)
                dve.wait_ge(route, r + 6)
                if b >= 1:
                    dve.wait_ge(pos_ready, b)
                nc.vector.tensor_tensor(run[:, (b + 1) % 2, :], run1[:, :], lab[:, b % 2, 1, :], ALU.add
                                        ).then_inc(route, 1)

            def destinations(b):
                dve.wait_ge(e01_done, b + 1)
                wr = S_WTS * b
                nc.vector.tensor_scalar(s01[:, :], e01[:, :], 1.0, None, ALU.add).then_inc(wts_done, 1)
                dve.wait_ge(wts_done, wr + 1)
                nc.vector.reciprocal(rows[:, b % 2, 0, :, D + 1], s01[:, :]).then_inc(wts_done, 1)
                dve.wait_ge(wts_done, wr + 2)
                nc.vector.tensor_tensor(rows[:, b % 2, 1, :, D + 1], rows[:, b % 2, 0, :, D + 1], e01[:, :], ALU.mult)
                for k in range(TOPK):
                    nc.vector.tensor_copy(rows[:, b % 2, k, :, D].bitcast(i32), dest_meta[:, 2 * b:2 * b + 2, k])
                dve.wait_ge(pos_ready, b + 1)
                pv = POS
                nc.vector.tensor_tensor(ohp[:, :, :].rearrange("p (t k) e -> p t k e", k=TOPK),
                                        bass.AP(tensor=pv.tensor, offset=pv.offset,
                                                ap=[pv.ap[0], [E, 2], [0, TOPK], [1, E]]),
                                        oh[:, :, :].rearrange("p (t k) e -> p t k e", k=TOPK),
                                        ALU.mult).then_inc(wts_done, 1)
                dve.wait_ge(wts_done, wr + 3)
                nc.vector.tensor_reduce(posk[:, :], ohp[:, :, :], axis=AX.X, op=ALU.add).then_inc(wts_done, 1)
                dve.wait_ge(wts_done, wr + 4)
                nc.vector.tensor_scalar(over[:, :], posk[:, :], float(CAP), float(NEVER), ALU.is_gt, ALU.mult)
                nc.vector.scalar_tensor_tensor(slotf[:, :], idxf[:, :], float(CAP), posk[:, :], ALU.mult, ALU.add
                                               ).then_inc(wts_done, 1)
                dve.wait_ge(wts_done, wr + 5)
                nc.vector.scalar_tensor_tensor(dest[:, b % 2, :], slotf[:, :], -1.0, over[:, :], ALU.add, ALU.add
                                               ).then_inc(dest_ready, 1)

            for U in range(-2, UNITS + 4):
                for g in range(UP):
                    if U + 2 < UNITS:
                        maxima(U + 2, g)
                    if g == 0 and U % 2 and 0 <= (U - 5) // 2 < B:
                        top_two((U - 5) // 2)
                    if g == 0 and U % 2 == 0 and 0 <= (U - 4) // 2 < B:
                        tokens_norm((U - 4) // 2)
                    if g == 1 and 0 <= U - 2 < UNITS:
                        normalize(U - 2)
                    if g == 1 and U % 2 == 0 and 0 <= (U - 4) // 2 < B:
                        tokens_out((U - 4) // 2)
                    if g == 1 and U % 2 and 0 <= (U - 5) // 2 < B:
                        destinations((U - 5) // 2)
                if U + 2 < UNITS:
                    split_maxima(U + 2)

            for e in range(E):
                for c in range(HC):
                    n = HC * e + c
                    dve.wait_ge(gate_done, n + 1)
                    if e >= 2 and c == 0:
                        dve.wait_ge(yo_ready, e - 1)
                    nc.vector.tensor_tensor(hid[:, e % 2, c, :], PS[:, 4 + n % 2, 0:CAP], gate[:, n % 2, :],
                                            ALU.mult).then_inc(hid_done, 1)
                dve.wait_ge(yo_ready, e + 1)
                if e >= 2:
                    dve.wait_ge(answered[e % 2], 16 * ST_TILES * (e // 2))
                for s in range(ST_TILES):
                    n = 128 if s < ST_TILES - 1 else LAST
                    c = nc.vector.tensor_scalar(yr[0:n, e % 2, s, :], PS[0:n, 6 + e % 2, 128 * s:128 * s + D],
                                                ex[0:n, e, s, D + 1:D + 2], None, ALU.mult)
                c.then_inc(yr_done, 1)
            for g in range(GROUPS):
                v = yy[:, 0, 4 * g:4 * g + 4, :]
                dve.wait_ge(yy_in[g], 32)
                nc.vector.tensor_tensor(v, v, yy[:, 1, 4 * g:4 * g + 4, :], ALU.add).then_inc(sum_done, 1)
                dve.wait_ge(sum_done, g + 1)
                xv = xs[:, 4 * g:4 * g + 4, :]
                nc.vector.scalar_tensor_tensor(xv, v, tgf[:, 0:1], xv, ALU.mult, ALU.add).then_inc(out_done, 1)

        @block.tensor
        def _(pe):
            def transpose4(src, bank):
                for i in range(4):
                    c = nc.tensor.transpose(PS[:, bank, 128 * i:128 * i + 128], src[:, i, :], ident[:, :])
                c.then_inc(tr_ready, 1)

            pe.wait_ge(consts, 2)
            pe.wait_ge(ctx_in, 16)
            transpose4(ctxs, 0)
            pe.wait_ge(w_in, 48)
            pe.wait_ge(hT_ready, 1)
            nc.tensor.matmul(PS[:, 4, :].rearrange("p (b m) -> p b m", m=M), wks[:, :], ctxT[:, :, 0:M],
                             start=True, stop=True).then_inc(k_ready, 1)
            for b in range(B):
                c = nc.tensor.matmul(PS[:, 6 if b < 4 else 2, 128 * (b % 4):128 * (b % 4) + 128], ctxT[:, b, :],
                                     wvs[:, :], start=True, stop=True)
            c.then_inc(v_ready, 1)
            for g in range(GROUPS):
                i = (g + 1) % 2
                pe.wait_ge(xn_ready, g + 1)
                transpose4(xn[g % 2], i)
                pe.wait_ge(hT_ready, g + 2)
                if g == 1:
                    pe.wait_ge(v_done, 1)
                if g >= 2:
                    pe.wait_ge(rq_done, g - 1)
                nc.tensor.matmul(PS[:, 2 + i, :], wqs[:, :], hT[g % 2], start=True, stop=True).then_inc(q_ready, 1)
                if g >= 1:
                    pe.wait_ge(rk_done, g)
                nc.tensor.matmul(PS[:, 4 + i, :], wks[:, :], hT[g % 2], start=True, stop=True).then_inc(k_ready, 1)
                if g >= 1:
                    pe.wait_ge(v_done, g)
                for t in range(4):
                    c = nc.tensor.matmul(PS[:, 6 + i, 128 * t:128 * t + 128], hT[g % 2][:, 128 * t:128 * t + 128],
                                         wvs[:, :], start=True, stop=True)
                c.then_inc(v_ready, 1)

            def scores(U, g, pieces):
                s, bb, g0 = place(U)
                if g == 0 and U % 4 == 0 and 0 in pieces:
                    pe.wait_ge(stack_in[U // 4], 16 * 24)
                    if U // 4 < RING:
                        pe.wait_ge(fixed_in[U // 4], 16 * 3)
                for piece in pieces:
                    n = 3 * (UP * U + g) + piece
                    if n >= 2:
                        pe.wait_ge(max_done, n - 1)
                    bank = PS[:, 4 + n % 2, :]
                    if piece == 0:
                        q = qst[0:MROW, s, g0 + g, bb, 0:128]
                        nc.tensor.matmul(bank[:, 0:128], q, kst[0:MROW, s, g0 + g, bb, 0:128], start=True, stop=False)
                        nc.tensor.matmul(bank[:, 128:384], q, kst[0:MROW, s, g0 + g, bb, N:2 * N],
                                         start=False, stop=False)
                        c = nc.tensor.matmul(bank[:, 0:512].rearrange("p (q k) -> p q k", q=2)[:, :, 0:128],
                                             identb[:, :], maskb[:, :, :], start=False, stop=True)
                    else:
                        par = piece - 1
                        own = 128 + M * par
                        nc.tensor.matmul(bank[:, 0:KEYS], qst[0:MROW, s, g0 + g, bb, 128:256],
                                         kst[0:MROW, s, g0 + g, bb, KEYS * par:KEYS * (par + 1)],
                                         start=True, stop=False)
                        c = nc.tensor.matmul(bank[:, own:own + 128], identb[:, :], maskb[:, 0, :],
                                             start=False, stop=True)
                    c.then_inc(s_ready, 1)

            def scores_t(U, g, par):
                s, bb, g0 = place(U)
                if g == 0 and par == 0:
                    pe.wait_ge(m_in[U % 2], 64 * (U // 2 + 1))
                q = qst[0:KROWS, s, g0 + g, bb, :]
                k = kst[0:KROWS, s, g0 + g, bb, :]
                odd = N + 2 * M
                k0 = odd * par
                n = 2 * (UP * U + g) + par
                if n >= 3:
                    pe.wait_ge(exp_done, n - 2)
                nc.tensor.matmul(PS[:, n % 3, 0:N], k[:, k0:k0 + 128], q, start=True, stop=True)
                nc.tensor.matmul(PS[:, n % 3, N:N + 128], k[:, k0 + 128:k0 + N], q[:, 128:N],
                                 start=True, stop=True)
                nc.tensor.matmul(PS[:, n % 3, N + 128:2 * N], k[:, N:odd], q[:, 128 * par:128 * par + 128],
                                 start=True, stop=True).then_inc(st_ready, 1)

            def values(V, chunk):
                b, g0 = V // 2, UP * (V % 2)
                if chunk == 0:
                    pe.wait_ge(exp_done, 2 * UP * (V + 1))
                    pe.wait_ge(vp_ready, b + 1)
                    if V >= 1:
                        pe.wait_ge(ot_done, V)
                if chunk == 1:
                    pe.wait_ge(sel_done, UP * V + UP)
                for par in {0: (None,), 1: (0,), 2: (1,), 3: (0, 1)}[chunk]:
                    for j in range(UP):
                        w = pt[:, V % 2, j, :].rearrange("p (e c) -> p e c", e=2)
                        if chunk == 0:
                            blk, q0, w = g0 + j, 0, w[:, :, N + 128:2 * N]
                        elif chunk < 3:
                            blk, q0, w = PAIRS + 2 * (g0 + j) + par, 0, w[:, par, 0:N]
                        else:
                            blk, q0, w = 3 * PAIRS + 2 * (g0 + j) + par, 128, w[:, par, N:N + 128]
                        c = nc.tensor.matmul(O[VW * j:VW * j + VW, q0:N], vp[:, b % 2, blk, :], w,
                                             start=(chunk == 0), stop=(chunk == 3 and par == 1))
                if chunk == 3:
                    c.then_inc(pv_done, 1)

            def maxima_t(U):
                pe.wait_ge(split_done, 2 * (U + 1))
                if U >= 1:
                    pe.wait_ge(mrow_done, U)
                if U >= 4:
                    pe.wait_ge(att_done, U - 3)
                for t in range(2):
                    c = nc.tensor.matmul(MT[:, 128 * t:128 * t + 128],
                                         mxb[:, U % 2, t, :, :].rearrange("p c r -> p (c r)"), identb[:, :],
                                         start=True, stop=True)
                c.then_inc(mT_ready, 1)

            def turn_values(V):
                pe.wait_ge(ot_done, V + 1)
                if V + 3 < UNITS:
                    pe.wait_ge(mrow_done, V + 4)
                if V >= 1:
                    pe.wait_ge(att_done, V)
                for t in range(2):
                    c = nc.tensor.transpose(PS[:, 7, 128 * t:128 * t + 128], ots[:, V % 2, 128 * t:128 * t + 128],
                                            ident[:, :])
                c.then_inc(oT_ready, 1)

            def turn_attention(b):
                pe.wait_ge(att_done, 2 * b + 2)
                if b >= 1:
                    pe.wait_ge(wts_done, S_WTS * (b - 1) + 3)
                for t in range(2):
                    c = nc.tensor.transpose(MISC[:, 128 * t:128 * t + 128], att[:, b % 2, t, :], ident[:, :])
                c.then_inc(attT_ready, 1)

            def project(b):
                pe.wait_ge(attT_done, b + 1)
                if b == 0:
                    pe.wait_ge(tanh_done, 1)
                for t in range(2):
                    nc.tensor.matmul(MISC[:, 128 * t:128 * t + 128], attT[:, 128 * t:128 * t + 128], wos[:, :],
                                     start=True, stop=False)
                    c = nc.tensor.matmul(MISC[:, 128 * t:128 * t + 128], onesf[:, :], bos[:, :],
                                         start=False, stop=True)
                c.then_inc(y_ready, 1)

            def turn_tokens(b):
                pe.wait_ge(h2_ready, b + 1)
                for t in range(2):
                    c = nc.tensor.transpose(MISC[:, 128 * t:128 * t + 128], rows[:, b % 2, 0, t, 0:D], ident[:, :])
                c.then_inc(h2T_ready, 1)

            def logits(b):
                pe.wait_ge(h2T_done, b + 1)
                for t in range(2):
                    c = nc.tensor.matmul(LOGITS[:, t, :], h2t[:, 128 * t:128 * t + 128], wgs[:, :],
                                         start=True, stop=True)
                c.then_inc(lg_ready, 1)

            def positions(b):
                pe.wait_ge(lab_ready, b + 1)
                pe.wait_ge(route, S_ROUTE * b)
                cur, rn = lab[:, b % 2, :, :], run[:, b % 2, :]
                nc.tensor.matmul(POS[:, 0, :], tri[:, :], cur[:, 0, :], start=True, stop=False)
                nc.tensor.matmul(POS[:, 0, :], ones[:, :], rn, start=False, stop=True)
                nc.tensor.matmul(POS[:, 1, :], tri[:, :], cur[:, 1, :], start=True, stop=False)
                nc.tensor.matmul(POS[:, 1, :], ones[:, :], cur[:, 0, :], start=False, stop=False)
                nc.tensor.matmul(POS[:, 1, :], ones[:, :], rn, start=False, stop=True).then_inc(pos_ready, 1)

            pe.wait_ge(consts, 13)
            pe.wait_ge(cast, 4)
            pe.wait_ge(q3_done, GROUPS)
            pe.wait_ge(k3_done, GROUPS)
            pe.wait_ge(v_done, GROUPS + 1)
            for U in range(-2, UNITS + 4):
                for g in range(UP):
                    for piece in range(3):
                        if U + 2 < UNITS:
                            scores(U + 2, g, (piece,))
                        if 0 <= U < UNITS and piece < 2:
                            scores_t(U, g, piece)
                    if g == 0 and -1 <= U and U + 1 < UNITS:
                        maxima_t(U + 1)
                    if 0 <= U - 1 < UNITS:
                        values(U - 1, g)
                    if g == 1 and U % 2 and 0 <= (U - 5) // 2 < B:
                        positions((U - 5) // 2)
                    if g == 1 and 0 <= U - 2 < UNITS:
                        turn_values(U - 2)
                    if g == 2 and U % 2 and 0 <= (U - 3) // 2 < B:
                        turn_attention((U - 3) // 2)
                    if g == 3 and U % 2 and 0 <= (U - 3) // 2 < B:
                        project((U - 3) // 2)
                    if g == 2 and U % 2 == 0 and 0 <= (U - 4) // 2 < B:
                        turn_tokens((U - 4) // 2)
                    if g == 3 and U % 2 == 0 and 0 <= (U - 4) // 2 < B:
                        logits((U - 4) // 2)

            def turn(e):
                pe.wait_ge(ex_in[e], 32)
                if e >= 2:
                    pe.wait_ge(xT_done, e - 1)
                for s in range(ST_TILES):
                    n = 128 if s < ST_TILES - 1 else LAST
                    c = nc.tensor.transpose(PS[:, e % 2, 128 * s:128 * s + n], ex[0:n, e, s, 0:D], ident[0:n, 0:n])
                c.then_inc(xT_ready, 1)

            def up(e):
                pe.wait_ge(wx_in[e % 2], 48 * (e // 2 + 1))
                pe.wait_ge(xT_done, e + 1)
                for c in range(HC):
                    n = HC * e + c
                    if n >= 2:
                        pe.wait_ge(hid_done, n - 1)
                    nc.tensor.matmul(PS[:, 2 + n % 2, 0:CAP], w1s[:, e % 2, 128 * c:128 * c + 128], xT[:, e % 2, :],
                                     start=True, stop=True)
                    nc.tensor.matmul(PS[:, 4 + n % 2, 0:CAP], w2s[:, e % 2, 128 * c:128 * c + 128], xT[:, e % 2, :],
                                     start=True, stop=True).then_inc(h_ready, 1)

            def down(e):
                pe.wait_ge(hid_done, HC * (e + 1))
                if e >= 2:
                    pe.wait_ge(yr_done, e - 1)
                for s in range(ST_TILES):
                    n = 128 if s < ST_TILES - 1 else LAST
                    for c in range(HC):
                        m = nc.tensor.matmul(PS[0:n, 6 + e % 2, 128 * s:128 * s + D],
                                             hid[:, e % 2, c, 128 * s:128 * s + n], w3s[:, e % 2, c, :],
                                             start=(c == 0), stop=(c == HC - 1))
                m.then_inc(yo_ready, 1)

            turn(0)
            for e in range(E):
                up(e)
                if e + 1 < E:
                    turn(e + 1)
                down(e)
        del block
    return nc


def x_tiles(ap):
    return ap.rearrange("b (t p) d -> p (b t) d", p=128)


def kernel(x, ctx_1024, g_xattn, g_ffn, L0_xattn_Wq, L0_xattn_Wkv, L0_xattn_Wout, L0_xattn_bout,
           L0_ffn_Wg, L0_ffn_bg, L0_ffn_W1, L0_ffn_W2, L0_ffn_W3):
    import numpy as _np
    import concourse.bacc as _bacc
    from concourse import mybir as _mybir
    from concourse.bass_utils import run_bass_kernel_spmd as _run

    def by_parity(w):
        return _np.asarray(w).reshape(128, 8, 2, 8).transpose(0, 2, 3, 1).reshape(128, 128)

    wkv = _np.asarray(L0_xattn_Wkv)
    ins = {"x": x, "ctx": ctx_1024, "g_xattn": g_xattn, "g_ffn": g_ffn, "wq": by_parity(L0_xattn_Wq),
           "wk": by_parity(wkv[:, :128]), "wv": wkv[:, 128:], "wout": L0_xattn_Wout, "bout": L0_xattn_bout,
           "wg": L0_ffn_Wg, "bg": L0_ffn_bg, "w1": L0_ffn_W1, "w2": L0_ffn_W2, "w3": L0_ffn_W3}
    nc = _bacc.Bacc("TRN2", target_bir_lowering=False, num_devices=1)
    arrays, args = {}, {}
    for name, a in ins.items():
        a = _np.ascontiguousarray(a)
        arrays[f"in_{name}"] = a
        args[name] = nc.dram_tensor(f"in_{name}", a.shape, _mybir.dt.from_np(a.dtype), kind="ExternalInput").ap()
    fp32 = _mybir.dt.float32
    args["slots_dram"] = nc.dram_tensor("slots", (8 * 320, 130), fp32, kind="Internal").ap()
    args["answers_dram"] = nc.dram_tensor("answers", (2 * 2048, 128), fp32, kind="Internal").ap()
    args["out"] = nc.dram_tensor("out_0", (8, 256, 128), fp32, kind="ExternalOutput").ap()
    flamingo_gated_block(nc, **args)
    r = _run(nc, [arrays], core_ids=[0])
    return r.results[0]["out_0"]
```

```python
import concourse.bass as bass
from concourse import mybir
from contextlib import ExitStack


def flamingo_gated_block(nc, x, ctx, g_xattn, g_ffn, wq, wk, wv, wout, bout, wg, bg, w1, w2, w3,
                         slots_dram, answers_dram, out):
    fp32, bf16 = mybir.dt.float32, mybir.dt.bfloat16
    i32, u32 = mybir.dt.int32, mybir.dt.uint32
    ALU = mybir.AluOpType
    ACT = mybir.ActivationFunctionType
    AX = mybir.AxisListType

    B, N, D = x.shape
    M = ctx.shape[1]
    HEADS, HD = 16, 8
    PAIRS = HEADS // 2
    UP = 4
    UNITS = 2 * B
    KEYS = M + N
    T = B * N
    TILES = T // 128
    GROUPS = TILES // 4
    E, _, H = w1.shape
    HC = H // 128
    TOPK = 2
    CAP = int(T / E * 1.25)
    SLOTS = E * CAP
    ST_TILES = (CAP + 127) // 128
    LAST = CAP - 128 * (ST_TILES - 1)
    SCALE = float(HD) ** -0.5
    RING = 3
    QROW = 6 * HD
    MROW = 2 * QROW
    KROWS = MROW + 4
    QPART = (0, 0, 0, 1, 1, 2)
    KPART = (0, 1, 2, 0, 1, 0)
    VW = 32
    ROW = D + 2
    NEVER = 1 << 22
    MASKED = -1e30
    EPS = 1e-5

    es = ExitStack()
    with es:
        def sb(name, shape, dt=fp32):
            return es.enter_context(nc.sbuf_tensor(name, shape, dt))

        def sem(name):
            return es.enter_context(nc.semaphore(name))

        PS = es.enter_context(nc.psum_tensor("PS", [128, 8, 512], fp32))

        xs = sb("xs", [128, TILES, D])
        kst = sb("kst", [128, RING, PAIRS, 2, 2 * KEYS], bf16)
        qst = sb("qst", [128, RING, PAIRS, 2, N], bf16)
        pt = sb("pt", [128, 2, UP, 1024])
        vraw = sb("vraw", [128, B, 3, D])
        vp = sb("vp", [128, 2, 5 * PAIRS, VW])
        kp = sb("kp", [128, GROUPS, 3, 2, KEYS + M], bf16)
        qp = sb("qp", [128, GROUPS, 3, 512], bf16)
        w1s = sb("w1s", [128, 2, H])
        w2s = sb("w2s", [128, 2, H])
        w3s = sb("w3s", [128, 2, HC, D])
        wqs = sb("wqs", [128, D])
        wks = sb("wks", [128, D])
        wvs = sb("wvs", [128, D])
        wos = sb("wos", [128, D])
        bos = sb("bos", [1, D])
        onesf = sb("onesf", [1, 128])
        wgs = sb("wgs", [128, E])
        bg2 = sb("bg2", [128, 2, E])
        gx = sb("gx", [128, 1])
        gf = sb("gf", [128, 1])
        tgx = sb("tgx", [128, 1])
        tgf = sb("tgf", [128, 1])
        ident = sb("ident", [128, 128])
        identb = sb("identb", [128, 128], bf16)
        maskb = sb("maskb", [128, 2, 128], bf16)
        tri = sb("tri", [128, 128], bf16)
        ones = sb("ones", [128, 128], bf16)
        half = sb("half", [128, 4])
        iotak = sb("iotak", [128, 4, E])
        dest_meta = sb("dest_meta", [128, TILES, 2], i32)
        blank = sb("blank", [128, ROW])
        stats = sb("stats", [128, 4, 6])
        mv = sb("mv", [128, GROUPS, 4, 2])
        veps = sb("veps", [128, GROUPS, 4])
        rstd = sb("rstd", [128, GROUPS, 4])
        mx = sb("mx", [128, 2, 2, 2, UP])
        mxb = sb("mxb", [128, 2, 2, 2, 2 * UP], bf16)
        mrow = sb("mrow", [4 * UP, 2, N], bf16)
        ots = sb("ots", [128, 2, N])
        rec = sb("rec", [128, 2, UP, 2])
        att = sb("att", [128, 2, 2, D])
        attT = sb("attT", [128, N])
        h2t = sb("h2t", [128, N])
        rows = sb("rows", [128, 2, TOPK, 2, ROW])
        lg = sb("lg", [128, 2, E])
        top = sb("top", [128, 2, 8])
        topi = sb("topi", [128, 2, 8], u32)
        idxf = sb("idxf", [128, 4])
        oh = sb("oh", [128, 4, E])
        lab = sb("lab", [128, 2, 2, E], bf16)
        run = sb("run", [128, 2, E], bf16)
        run1 = sb("run1", [128, E], bf16)
        d01 = sb("d01", [128, 2])
        e01 = sb("e01", [128, 2])
        s01 = sb("s01", [128, 2])
        ohp = sb("ohp", [128, 4, E])
        posk = sb("posk", [128, 4])
        over = sb("over", [128, 4])
        slotf = sb("slotf", [128, 4])
        dest = sb("dest", [128, 2, 4], u32)

        ptf = pt[:, :, :, :].rearrange("p a b c -> p (a b c)")
        zeros = ptf[:, 0:1024]
        xn = [ptf[:, 1024 + 512 * i:1536 + 512 * i].rearrange("p (t d) -> p t d", d=D) for i in range(2)]
        hT = [ptf[:, 2048 + 512 * i:2560 + 512 * i] for i in range(2)]
        ctxT = ptf[:, 3072:4096].rearrange("p (b c) -> p b c", c=128)
        ctxs = ptf[:, 4096:4608].rearrange("p (t d) -> p t d", d=D)
        rq = [ptf[:, 4608 + 512 * i:5120 + 512 * i] for i in range(2)]
        rk = [ptf[:, 5632 + 512 * i:6144 + 512 * i] for i in range(2)]

        zrow = ptf[0:QROW, 6656:6656 + KEYS // 2].bitcast(bf16)
        frow = ptf[0:4, 6656 + KEYS // 2:6656 + 3 * KEYS // 2].bitcast(bf16).rearrange("p (a k) -> p a k", a=2)

        kf = kst[:, :, :, :, :].rearrange("p a b c d -> p (a b c d)").bitcast(fp32)
        o = 0

        def room(n):
            nonlocal o
            o += n
            return kf[:, o - n:o]

        ex = room(E * ST_TILES * ROW).rearrange("p (e s c) -> p e s c", e=E, s=ST_TILES)
        xT = room(2 * CAP).rearrange("p (a c) -> p a c", a=2)
        gate = room(2 * CAP).rearrange("p (a c) -> p a c", a=2)
        hid = room(2 * HC * CAP).rearrange("p (a h c) -> p a h c", a=2, h=HC)
        yr = room(2 * ST_TILES * D).rearrange("p (a s d) -> p a s d", a=2, s=ST_TILES)
        qf = qst[:, :, :, :, :].rearrange("p a b c d -> p (a b c d)").bitcast(fp32)
        yy = qf[:, 0:TOPK * TILES * D].rearrange("p (k t d) -> p k t d", k=TOPK, t=TILES)

        w_in = sem("w_in")
        x_in = [sem(f"x_in{g}") for g in range(GROUPS)]
        ctx_in = sem("ctx_in")
        small_in = sem("small_in")
        zeroed = sem("zeroed")
        fixed_in = [sem(f"fixed_in{s}") for s in range(RING)]
        consts = sem("consts")
        cast = sem("cast")
        dram_zero = sem("dram_zero")
        stat = sem("stat")
        eps_added = sem("eps_added")
        rstd_ready = sem("rstd_ready")
        xn_ready = sem("xn_ready")
        tr_ready = sem("tr_ready")
        hT_ready = sem("hT_ready")
        q_ready = sem("q_ready")
        k_ready = sem("k_ready")
        v_ready = sem("v_ready")
        q1_done = sem("q1_done")
        k1_done = sem("k1_done")
        rq_done = sem("rq_done")
        rk_done = sem("rk_done")
        q2_done = sem("q2_done")
        k2_done = sem("k2_done")
        q3_done = sem("q3_done")
        k3_done = sem("k3_done")
        ctx_done = sem("ctx_done")
        v_done = sem("v_done")
        stack_in = [sem(f"stack_in{g}") for g in range(GROUPS)]
        s_ready = sem("s_ready")
        max_done = sem("max_done")
        split_done = sem("split_done")
        mT_ready = sem("mT_ready")
        mrow_done = sem("mrow_done")
        m_in = [sem(f"m_in{i}") for i in range(2)]
        st_ready = sem("st_ready")
        exp_done = sem("exp_done")
        sel_done = sem("sel_done")
        vp_ready = sem("vp_ready")
        pv_done = sem("pv_done")
        ot_done = sem("ot_done")
        oT_ready = sem("oT_ready")
        rec_done = sem("rec_done")
        att_done = sem("att_done")
        attT_ready = sem("attT_ready")
        attT_done = sem("attT_done")
        y_ready = sem("y_ready")
        x1_done = sem("x1_done")
        tanh_done = sem("tanh_done")
        h2_ready = sem("h2_ready")
        h2T_ready = sem("h2T_ready")
        h2T_done = sem("h2T_done")
        row1_done = sem("row1_done")
        lg_ready = sem("lg_ready")
        route = sem("route")
        lab_ready = sem("lab_ready")
        d01_ready = sem("d01_ready")
        e01_done = sem("e01_done")
        pos_ready = sem("pos_ready")
        wts_done = sem("wts_done")
        dest_ready = sem("dest_ready")
        sent = [sem(f"sent{i}") for i in range(2)]
        wx_in = [sem(f"wx_in{i}") for i in range(2)]
        w3_in = [sem(f"w3_in{i}") for i in range(2)]
        ex_in = [sem(f"ex_in{e}") for e in range(E)]
        xT_ready = sem("xT_ready")
        xT_done = sem("xT_done")
        h_ready = sem("h_ready")
        gate_done = sem("gate_done")
        hid_done = sem("hid_done")
        yo_ready = sem("yo_ready")
        yr_done = sem("yr_done")
        answered = [sem(f"answered{i}") for i in range(2)]
        yy_in = [sem(f"yy_in{g}") for g in range(GROUPS)]
        sum_done = sem("sum_done")
        out_done = sem("out_done")
        stored = sem("stored")

        S_ROUTE = 7
        S_WTS = 5
        S_STAT = 8
        MT = PS[0:4 * UP, 7, N:2 * N]
        OT = PS[:, 7, 0:N].rearrange("p (t j c) -> p t j c", t=2, j=UP)
        STEPS = 3 * UP
        S_BANKS = (4, 5, 2)
        MISC = PS[:, 3, 0:N]
        LOGITS = PS[:, 3, 0:2 * E].rearrange("p (t e) -> p t e", e=E)
        POS = PS[:, 3, 2 * E:4 * E].rearrange("p (t e) -> p t e", e=E)
        O = PS[:, 6, 0:N]

        def place(U):
            b = U // 2
            return (b // 2) % RING, b % 2, UP * (U % 2)

        block = es.enter_context(nc.Block())

        @block.sync
        def _(sp):
            sp.dma_start(xs[:, 0:4, :], x_tiles(x)[:, 0:4, :]).then_inc(x_in[0], 16)
            for w, s in ((wq, wqs), (wk, wks), (wv, wvs)):
                sp.dma_start(s[:, :], w).then_inc(w_in, 16)
            for g in range(1, GROUPS):
                sp.dma_start(xs[:, 4 * g:4 * g + 4, :], x_tiles(x)[:, 4 * g:4 * g + 4, :]).then_inc(x_in[g], 16)
            for s, w in ((gx, g_xattn.partition_broadcast(128)), (gf, g_ffn.partition_broadcast(128)), (wgs, wg),
                         (bg2[:, 0, :], bg.partition_broadcast(128)), (bg2[:, 1, :], bg.partition_broadcast(128)),
                         (wos, wout), (bos, bout.rearrange("(a n) -> a n", a=1))):
                sp.dma_start(s[:, :], w).then_inc(small_in, 16)

            def load_q(g, par, r):
                row = QROW * par + HD * r
                sp.wait_ge((q1_done, q2_done, q3_done)[QPART[r]], g + 1)
                sp.dma_start(qst[row:row + HD, g % RING, :, :, :].rearrange("p g b n -> p g (b n)"),
                             qp[64 * par:64 * par + 64, g, QPART[r], :]).then_inc(stack_in[g], 16)

            def load_k(g, par, r):
                row = QROW * par + HD * r
                if KPART[r] < 2:
                    sp.wait_ge((k1_done, k2_done)[KPART[r]], g + 2)
                else:
                    sp.wait_ge(k3_done, g + 1)
                sp.wait_ge(ctx_done, 1)
                sp.dma_start(kst[row:row + HD, g % RING, :, :, KEYS * par:KEYS * (par + 1)],
                             kp[64 * par:64 * par + 64, g, KPART[r], :, M * (1 - par):M * (1 - par) + KEYS]
                             ).then_inc(stack_in[g], 16)

            def load_quarter(g, quarter):
                for r in range(6):
                    (load_q, load_k)[quarter // 2](g, quarter % 2, r)

            def load_maxima(U):
                s, bb, g0 = place(U)
                sp.wait_ge(mrow_done, U + 1)
                for par in range(2):
                    for part in range(2):
                        row = MROW + 2 * par + part
                        sp.dma_start(qst[row:row + 1, s, g0:g0 + UP, bb, :],
                                     mrow[UP * (2 * part + par):UP * (2 * part + par + 1), U % 2, :]).then_inc(m_in[U % 2], 16)

            def load_expert(e):
                if e >= 2:
                    sp.wait_ge(h_ready, HC * (e - 1))
                sp.dma_start(w1s[:, e % 2, :], w1[e]).then_inc(wx_in[e % 2], 16)
                sp.dma_start(w2s[:, e % 2, :], w2[e]).then_inc(wx_in[e % 2], 16)
                if e >= 2:
                    sp.wait_ge(yo_ready, e - 1)
                sp.dma_start(w3s[:, e % 2, :, :], w3[e].rearrange("(c p) d -> p c d", p=128)
                             ).then_inc(w3_in[e % 2], 16)

            sp.wait_ge(zeroed, 1)
            for s in range(RING):
                for rows_, k0, src in ((slice(0, QROW), KEYS, zrow), (slice(QROW, MROW), 0, zrow)):
                    sp.dma_start(kst[rows_, s, :, :, k0:k0 + KEYS].rearrange("p g b k -> p (g b) k"),
                                 bass.AP(tensor=src.tensor, offset=src.offset,
                                         ap=[src.ap[0], [0, 2 * PAIRS], [1, KEYS]])).then_inc(fixed_in[s], 16)
                src = frow[:, :, :]
                sp.dma_start(kst[MROW:KROWS, s, :, :, :].rearrange("p g b k -> p (g b) k"),
                             bass.AP(tensor=src.tensor, offset=src.offset,
                                     ap=[src.ap[0], [0, 2 * PAIRS], [1, 2 * KEYS]])).then_inc(fixed_in[s], 16)
            for part in range(3):
                for load, parts_ in ((load_q, QPART), (load_k, KPART)):
                    for r in range(6):
                        if parts_[r] == part:
                            load(0, 0, r)
                            load(0, 1, r)
            load_quarter(1, 0)
            load_quarter(1, 1)
            for U in range(UNITS):
                load_maxima(U)
                if U < 2:
                    load_quarter(1, 2 + U)
                elif U < 6:
                    load_quarter(2, U - 2)
                elif U < 10:
                    if U == 6:
                        sp.wait_ge(st_ready, 4 * 2 * UP)
                    load_quarter(RING, U - 6)
                if U == 10:
                    load_expert(0)
                    load_expert(1)
            for i in range(2):
                sp.wait_ge(sent[i], 16 * 4 * B // 2)
            sp.wait_ge(st_ready, 2 * UP * UNITS)
            for e in range(E):
                r0 = e * CAP
                sp.dma_start(ex[:, e, 0:ST_TILES - 1, :],
                             slots_dram[r0:r0 + 128 * (ST_TILES - 1), :].rearrange("(s p) c -> p s c", p=128)
                             ).then_inc(ex_in[e], 16)
                sp.dma_start(ex[0:LAST, e, ST_TILES - 1, :],
                             slots_dram[r0 + 128 * (ST_TILES - 1):r0 + CAP, :]).then_inc(ex_in[e], 16)
            for e in range(2, E):
                load_expert(e)
            for i in range(2):
                sp.wait_ge(answered[i], 16 * ST_TILES * E // 2)
            av = answers_dram.rearrange("(k t p) d -> k p t d", k=TOPK, p=128)
            for g in range(GROUPS):
                for k in range(TOPK):
                    sp.dma_start(yy[:, k, 4 * g:4 * g + 4, :], av[k, :, 4 * g:4 * g + 4, :]).then_inc(yy_in[g], 16)
            for g in range(GROUPS):
                sp.wait_ge(out_done, g + 1)
                sp.dma_start(x_tiles(out)[:, 4 * g:4 * g + 4, :], xs[:, 4 * g:4 * g + 4, :]).then_inc(stored, 16)
            sp.wait_ge(stored, 16 * GROUPS)

        @block.gpsimd
        def _(pool):
            nc.gpsimd.memset(ident[:, :], 0.0).then_inc(consts, 1)
            pool.wait_ge(consts, 1)
            nc.gpsimd.affine_select(out=ident[:, :], in_=ident[:, :], compare_op=ALU.not_equal, fill=1.0, base=0,
                                    pattern=[[-1, 128]], channel_multiplier=1).then_inc(consts, 1)
            nc.gpsimd.memset(half[:, :], -0.5).then_inc(consts, 1)
            nc.gpsimd.memset(maskb[:, :, :], 0.0).then_inc(consts, 1)
            nc.gpsimd.memset(onesf[:, :], 1.0).then_inc(consts, 1)
            nc.gpsimd.memset(ones[:, :], 1.0).then_inc(consts, 1)
            nc.gpsimd.memset(zeros, 0.0).then_inc(consts, 1)
            nc.gpsimd.memset(blank[:, :], 0.0).then_inc(consts, 1)
            pool.wait_ge(consts, 8)
            nc.gpsimd.affine_select(out=maskb[:, :, :], in_=maskb[:, :, :], compare_op=ALU.is_ge, fill=MASKED, base=0,
                                    pattern=[[0, 2], [-1, 128]], channel_multiplier=1).then_inc(consts, 1)
            nc.gpsimd.affine_select(out=tri[:, :], in_=ones[:, :], compare_op=ALU.is_ge, fill=0.0, base=0,
                                    pattern=[[1, 128]], channel_multiplier=-1).then_inc(consts, 1)
            nc.gpsimd.iota(iotak[:, :, :], pattern=[[0, 4], [1, E]], base=0, channel_multiplier=0,
                           allow_small_or_imprecise_dtypes=True).then_inc(consts, 1)
            nc.gpsimd.iota(dest_meta[:, :, :], pattern=[[128, TILES], [T, 2]], base=0,
                           channel_multiplier=1).then_inc(consts, 1)
            nc.gpsimd.iota(blank[:, D:D + 1].bitcast(i32), pattern=[[0, 1]], base=NEVER,
                           channel_multiplier=0).then_inc(consts, 1)

            pool.wait_ge(consts, 13)
            def rstd_of(n, par, count, stats_by):
                pool.wait_ge(stat, stats_by)
                nc.gpsimd.tensor_scalar(veps[:, par, 0:count], mv[:, par, 0:count, 1], 1.0, EPS, ALU.mult,
                                        ALU.add).then_inc(eps_added, 1)
                pool.wait_ge(eps_added, n + 1)
                nc.gpsimd.tensor_tensor(rstd[:, par, 0:count], veps[:, par, 0:count], half[:, 0:count],
                                        ALU.pow).then_inc(rstd_ready, 1)

            def third_parts(g):
                i = (g + 1) % 2
                pool.wait_ge(q2_done, g + 1)
                nc.gpsimd.tensor_tensor(qp[:, g, 2, :], rq[g % 2], qp[:, g, 1, :], ALU.subtract
                                        ).then_inc(q3_done, 1)
                pool.wait_ge(k2_done, g + 2)
                nc.gpsimd.tensor_tensor(kp[:, g, 2, :, M:KEYS], rk[i].rearrange("p (b n) -> p b n", b=2),
                                        kp[:, g, 1, :, M:KEYS], ALU.subtract).then_inc(k3_done, 1)

            def norm_batch(b):
                rstd_of(GROUPS + b, b % 2, 2, S_STAT * GROUPS + 4 * (b + 1))

            for g in range(GROUPS):
                rstd_of(g, g, 4, S_STAT * (g + 1))
            av = answers_dram.rearrange("(z p n) d -> z p (n d)", z=4, p=128)
            for z in range(4):
                nc.gpsimd.dma_start(av[z], zeros).then_inc(dram_zero, 16)
            bv = blank[:, :]
            nc.gpsimd.dma_start(slots_dram.rearrange("(n p) c -> p n c", p=128),
                                bass.AP(tensor=bv.tensor, offset=bv.offset,
                                        ap=[bv.ap[0], [0, SLOTS // 128], [1, ROW]])).then_inc(dram_zero, 16)

            for g in range(GROUPS):
                third_parts(g)
            for U in range(UNITS + 4):
                if U < UNITS:
                    for g in range(UP):
                        pool.wait_ge(exp_done, 2 * (UP * U + g + 1))
                        v = pt[:, U % 2, g, :].rearrange("p (s c) -> p s c", s=4)[:, :, 0:128]
                        nc.gpsimd.affine_select(out=v, in_=v, compare_op=ALU.is_ge, fill=0.0, base=0,
                                                pattern=[[0, 4], [1, 128]],
                                                channel_multiplier=-1).then_inc(sel_done, 1)
                if U % 2 and 0 <= (U - 3) // 2 < B:
                    norm_batch((U - 3) // 2)
                if U % 2 and 0 <= (U - 5) // 2 < B:
                    b = (U - 5) // 2
                    if b == 0:
                        pool.wait_ge(dram_zero, 16 * 5)
                    pool.wait_ge(dest_ready, b + 1)
                    pool.wait_ge(row1_done, b + 1)
                    for k in range(TOPK):
                        for t in range(2):
                            nc.gpsimd.indirect_dma_start(
                                out=slots_dram, out_offset=bass.IndirectOffsetOnAxis(
                                    ap=dest[:, b % 2, 2 * t + k:2 * t + k + 1], axis=0),
                                in_=rows[:, b % 2, k, t, :], in_offset=None,
                                bounds_check=SLOTS - 1, oob_is_err=False).then_inc(sent[b % 2], 16)
            for e in range(E):
                for s in range(ST_TILES):
                    pool.wait_ge(yr_done, ST_TILES * e + s + 1)
                    n = 128 if s < ST_TILES - 1 else LAST
                    nc.gpsimd.indirect_dma_start(
                        out=answers_dram, out_offset=bass.IndirectOffsetOnAxis(
                            ap=ex[0:n, e, s, D:D + 1].bitcast(u32), axis=0),
                        in_=yr[0:n, e % 2, s, :], in_offset=None,
                        bounds_check=TOPK * T - 1, oob_is_err=False).then_inc(answered[e % 2], 16)

        @block.scalar
        def _(act):
            act.dma_start(ctxs, ctx.rearrange("b m d -> (b m) d").rearrange("(t p) d -> p t d", p=128)
                          ).then_inc(ctx_in, 16)

            act.wait_ge(tr_ready, 1)
            v = PS[:, 0, :].rearrange("p (b m) -> p b m", m=M)
            nc.scalar.copy(ctxT[:, :, 0:M], v)
            nc.scalar.copy(ctxT[:, :, M:2 * M], v).then_inc(hT_ready, 1)
            act.wait_ge(k_ready, 1)
            kc = PS[:, 4, :].rearrange("p (g b m) -> p g b m", g=GROUPS, b=2)
            nc.scalar.copy(kp[:, :, 0, :, 0:M], kc).then_inc(k1_done, 1)
            act.wait_ge(v_ready, 1)
            nc.scalar.copy(vraw[:, 0:4, 0, :], PS[:, 6, :].rearrange("p (b d) -> p b d", d=D))
            nc.scalar.copy(vraw[:, 4:8, 0, :], PS[:, 2, :].rearrange("p (b d) -> p b d", d=D)).then_inc(v_done, 1)
            act.wait_ge(rk_done, 1)
            nc.scalar.copy(kp[:, :, 1, :, 0:M], rk[0].rearrange("p (g b m) -> p g b m", g=GROUPS, b=2)
                           ).then_inc(k2_done, 1)

            def tokens_turned(g):
                act.wait_ge(tr_ready, g + 2)
                if g >= 2:
                    act.wait_ge(v_ready, g)
                nc.scalar.copy(hT[g % 2], PS[:, (g + 1) % 2, :]).then_inc(hT_ready, 1)

            tokens_turned(0)
            for g in range(GROUPS):
                i = (g + 1) % 2
                if g + 1 < GROUPS:
                    tokens_turned(g + 1)
                act.wait_ge(q_ready, g + 1)
                nc.scalar.copy(qp[:, g, 0, :], PS[:, 2 + i, :]).then_inc(q1_done, 1)
                act.wait_ge(k_ready, g + 2)
                nc.scalar.copy(kp[:, g, 0, :, M:KEYS], PS[:, 4 + i, :].rearrange("p (b n) -> p b n", b=2)
                               ).then_inc(k1_done, 1)
                act.wait_ge(v_ready, g + 2)
                nc.scalar.copy(vraw[:, 2 * g:2 * g + 2, 1:3, :],
                               PS[:, 6 + i, :].rearrange("p (b t d) -> p b t d", b=2, t=2)).then_inc(v_done, 1)
                act.wait_ge(rq_done, g + 1)
                nc.scalar.copy(qp[:, g, 1, :], rq[g % 2]).then_inc(q2_done, 1)
                act.wait_ge(rk_done, g + 2)
                nc.scalar.copy(kp[:, g, 1, :, M:KEYS], rk[i].rearrange("p (b n) -> p b n", b=2)
                               ).then_inc(k2_done, 1)
            act.wait_ge(small_in, 16 * 7)
            nc.scalar.activation(tgx[:, :], gx[:, :], ACT.Tanh)
            nc.scalar.activation(tgf[:, :], gf[:, :], ACT.Tanh).then_inc(tanh_done, 1)

            def maxima_row(U):
                act.wait_ge(mT_ready, U + 1)
                if U >= 2:
                    act.wait_ge(m_in[U % 2], 64 * (U // 2))
                nc.scalar.copy(mrow[:, U % 2, :], MT).then_inc(mrow_done, 1)

            def pad_values(b):
                if b == 0:
                    act.wait_ge(v_done, GROUPS + 1)
                if b >= 2:
                    act.wait_ge(pv_done, 2 * b - 2)
                for par in range(2):
                    lo = vraw[64 * par:64 * par + 64, b, 0, :].rearrange("p (g q d) -> p g q d", q=2, d=HD)
                    c0 = 9 * par
                    nc.scalar.copy(vp[64 * par:64 * par + 64, b % 2, 0:PAIRS, c0:c0 + HD], lo[:, :, par, :])
                    for blk in range(2):
                        dst = vp[:, b % 2, PAIRS * (1 + 2 * blk):PAIRS * (3 + 2 * blk), :].rearrange(
                            "p (g q) c -> p g q c", q=2)
                        src = vraw[:, b, 1 + blk, :].rearrange("p (g q d) -> p g q d", q=2, d=HD)
                        ins = nc.scalar.copy(dst[:, :, par, c0:c0 + HD], src[:, :, par, :])
                ins.then_inc(vp_ready, 1)

            maxima_row(0)
            for U in range(UNITS + 4):
                if U >= 2 and U - 2 < UNITS:
                    V = U - 2
                    act.wait_ge(pv_done, V + 1)
                    if V >= 2:
                        act.wait_ge(oT_ready, V - 1)
                    nc.scalar.copy(ots[:, V % 2, :], O).then_inc(ot_done, 1)
                if U == 0:
                    act.wait_ge(dram_zero, 16 * 5)
                    act.wait_ge(q3_done, GROUPS)
                    act.wait_ge(k3_done, GROUPS)
                    act.wait_ge(ctx_done, 1)
                    act.wait_ge(v_ready, GROUPS + 1)
                    for s in range(RING):
                        act.wait_ge(fixed_in[s], 16 * 3)
                if 2 <= U < UNITS:
                    act.wait_ge(pv_done, U - 1)
                if U % 2 and 0 <= (U - 5) // 2 < B:
                    b = (U - 5) // 2
                    act.wait_ge(d01_ready, b + 1)
                    nc.scalar.activation(e01[:, :], d01[:, :], ACT.Exp).then_inc(e01_done, 1)
                for half_ in range(2 * UP):
                    if half_ == 4 and U % 2 and 0 <= (U - 3) // 2 < B:
                        b = (U - 3) // 2
                        act.wait_ge(attT_ready, b + 1)
                        if b >= 1:
                            act.wait_ge(y_ready, b)
                        nc.scalar.copy(attT[:, :], MISC).then_inc(attT_done, 1)
                    if half_ == 3 and U % 2 == 0 and 0 <= (U - 4) // 2 < B:
                        b = (U - 4) // 2
                        act.wait_ge(h2T_ready, b + 1)
                        nc.scalar.copy(h2t[:, :], MISC).then_inc(h2T_done, 1)
                        if b >= 2:
                            act.wait_ge(sent[b % 2], 16 * 4 * (b // 2))
                        nc.scalar.copy(rows[:, b % 2, 1, :, 0:D], rows[:, b % 2, 0, :, 0:D]).then_inc(row1_done, 1)
                    if half_ == 5 and U % 2 == 0 and U // 2 < B:
                        pad_values(U // 2)
                    if U < UNITS:
                        n = 2 * UP * U + half_
                        g, par = half_ // 2, half_ % 2
                        act.wait_ge(st_ready, n + 1)
                        nc.scalar.activation(pt[:, U % 2, g, 512 * par:512 * par + 512], PS[:, n % 2, :],
                                             ACT.Exp, scale=SCALE).then_inc(exp_done, 1)
                    if half_ == 0 and U + 1 < UNITS:
                        maxima_row(U + 1)

            def tokens_in(e):
                act.wait_ge(xT_ready, e + 1)
                if e >= 2:
                    act.wait_ge(h_ready, HC * (e - 1))
                nc.scalar.copy(xT[:, e % 2, :], PS[:, e % 2, 0:CAP]).then_inc(xT_done, 1)

            tokens_in(0)
            for e in range(E):
                for c in range(HC):
                    n = HC * e + c
                    if c == HC - 1 and e + 1 < E:
                        tokens_in(e + 1)
                    act.wait_ge(h_ready, n + 1)
                    if n >= 2:
                        act.wait_ge(hid_done, n - 1)
                    nc.scalar.activation(gate[:, n % 2, :], PS[:, 2 + n % 2, 0:CAP], ACT.Silu).then_inc(gate_done, 1)

        @block.vector
        def _(dve):
            nc.vector.memset(zrow, 0.0)
            nc.vector.memset(frow[:, 0, :], 0.0)
            nc.vector.memset(frow[:, 1, :], -1.0).then_inc(cast, 1)
            dve.wait_ge(cast, 1)
            nc.vector.memset(frow[0:2, 0, :], -1.0)
            nc.vector.memset(frow[0:2, 1, :], 0.0).then_inc(zeroed, 1)

            def norm_tokens(g):
                dve.wait_ge(rstd_ready, g + 1)
                if g >= 2:
                    dve.wait_ge(tr_ready, g)
                for i in range(4):
                    c = nc.vector.tensor_scalar(xn[g % 2][:, i, :], xs[:, 4 * g + i, :], mv[:, g, i, 0:1],
                                                rstd[:, g, i:i + 1], ALU.subtract, ALU.mult)
                c.then_inc(xn_ready, 1)

            def ctx_parts():
                dve.wait_ge(k1_done, 1)
                kc = PS[:, 4, :].rearrange("p (g b m) -> p g b m", g=GROUPS, b=2)
                rv = rk[0].rearrange("p (g b m) -> p g b m", g=GROUPS, b=2)
                nc.vector.tensor_tensor(rv, kc, kp[:, :, 0, :, 0:M], ALU.subtract).then_inc(rk_done, 1)
                dve.wait_ge(k2_done, 1)
                nc.vector.tensor_tensor(kp[:, :, 2, :, 0:M], rv, kp[:, :, 1, :, 0:M], ALU.subtract
                                        ).then_inc(cast, 1)
                dve.wait_ge(cast, 2)
                allp = kp[:, :, :, :, :].rearrange("p g c b k -> p (g c b) k")
                nc.vector.tensor_copy(allp[:, :, KEYS:KEYS + M], allp[:, :, 0:M]).then_inc(ctx_done, 1)

            def parts(g):
                i = (g + 1) % 2
                dve.wait_ge(q1_done, g + 1)
                if g >= 2:
                    dve.wait_ge(q3_done, g - 1)
                nc.vector.tensor_tensor(rq[g % 2], PS[:, 2 + i, :], qp[:, g, 0, :], ALU.subtract
                                        ).then_inc(rq_done, 1)
                dve.wait_ge(k1_done, g + 2)
                if g >= 2:
                    dve.wait_ge(k3_done, g - 1)
                nc.vector.tensor_tensor(rk[i].rearrange("p (b n) -> p b n", b=2),
                                        PS[:, 4 + i, :].rearrange("p (b n) -> p b n", b=2),
                                        kp[:, g, 0, :, M:KEYS], ALU.subtract).then_inc(rk_done, 1)

            def stats_group(g):
                dve.wait_ge(x_in[g], 16)
                if g >= 1:
                    dve.wait_ge(stat, S_STAT * g)
                for i in range(4):
                    nc.vector.bn_stats(stats[:, i, :], xs[:, 4 * g + i, :]).then_inc(stat, 1)
                for i in range(4):
                    dve.wait_ge(stat, S_STAT * g + i + 1)
                    nc.vector.bn_aggr(mv[:, g, i, :], stats[:, i, :]).then_inc(stat, 1)

            for g in range(GROUPS):
                stats_group(g)
                if g == 1:
                    norm_tokens(0)
                if g == 2:
                    norm_tokens(1)
            ctx_parts()
            for g in range(GROUPS):
                if 1 <= g < GROUPS - 1:
                    norm_tokens(g + 1)
                parts(g)
            nc.vector.memset(vp[:, :, :, :].rearrange("p a b c -> p (a b c)"), 0.0).then_inc(cast, 1)
            dve.wait_ge(cast, 3)
            nc.vector.memset(vp[0:64, :, 0:PAIRS, 8:9], 1.0)
            nc.vector.memset(vp[64:128, :, 0:PAIRS, 17:18], 1.0)
            for par in range(2):
                v = vp[:, :, PAIRS:5 * PAIRS, :].rearrange("p a (g q) c -> p a g q c", q=2)
                nc.vector.memset(v[:, :, :, par, 8 + 9 * par:9 + 9 * par], 1.0)
            dve.wait_ge(consts, 13)
            nc.vector.tensor_copy(identb[:, :], ident[:, :])
            nc.vector.memset(run[:, 0, :], 0.0).then_inc(cast, 1)

            def maxima(U, step):
                g, piece = step // 3, step % 3
                n = STEPS * U + step
                bank = PS[:, S_BANKS[n % 3], :]
                dve.wait_ge(s_ready, n + 1)
                if piece == 0:
                    nc.vector.tensor_reduce(mx[:, U % 2, 0, :, g],
                                            bank[:, 0:2 * (M + 128)].rearrange("p (q k) -> p q k", q=2),
                                            axis=AX.X, op=ALU.max).then_inc(max_done, 1)
                else:
                    nc.vector.tensor_reduce(mx[:, U % 2, 1, piece - 1, g:g + 1], bank[:, 0:KEYS],
                                            axis=AX.X, op=ALU.max).then_inc(max_done, 1)

            def split_maxima(U):
                dve.wait_ge(max_done, 3 * UP * (U + 1))
                if U >= 2:
                    dve.wait_ge(mT_ready, U - 1)
                m = mx[:, U % 2, :, :, :].rearrange("p t q g -> p t (q g)")
                nc.vector.tensor_copy(mxb[:, U % 2, :, 0, :], m).then_inc(split_done, 1)
                dve.wait_ge(split_done, 2 * U + 1)
                nc.vector.tensor_tensor(mxb[:, U % 2, :, 1, :], m, mxb[:, U % 2, :, 0, :], ALU.subtract
                                        ).then_inc(split_done, 1)

            def invert(V):
                dve.wait_ge(oT_ready, V + 1)
                nc.vector.reciprocal(rec[:, :, :, :], OT[:, :, :, HD:2 * HD + 2:HD + 1]).then_inc(rec_done, 1)

            def normalize(V):
                b, g0 = V // 2, UP * (V % 2)
                dve.wait_ge(rec_done, V + 1)
                if b >= 2 and V % 2 == 0:
                    dve.wait_ge(attT_ready, b - 1)
                for t in range(2):
                    rv = rec[:, t, :, :]
                    c = nc.vector.tensor_tensor(
                        att[:, b % 2, t, 2 * HD * g0:2 * HD * (g0 + UP)].rearrange("p (j q d) -> p j q d", q=2, d=HD),
                        OT[:, t, :, 0:2 * HD + 2].rearrange("p j (q d) -> p j q d", q=2)[:, :, :, 0:HD],
                        bass.AP(tensor=rv.tensor, offset=rv.offset, ap=[rv.ap[0], [2, UP], [1, 2], [0, HD]]),
                        ALU.mult)
                c.then_inc(att_done, 1)

            def tokens_norm(b, step):
                base = S_STAT * GROUPS + 4 * b
                if step == 0:
                    dve.wait_ge(y_ready, b + 1)
                    if b == 0:
                        dve.wait_ge(tanh_done, 1)
                    v = xs[:, 2 * b:2 * b + 2, :]
                    nc.vector.scalar_tensor_tensor(v, MISC.rearrange("p (t d) -> p t d", t=2), tgx[:, 0:1], v,
                                                   ALU.mult, ALU.add).then_inc(x1_done, 1)
                if step == 1:
                    dve.wait_ge(x1_done, b + 1)
                    for i in range(2):
                        nc.vector.bn_stats(stats[:, i, :], xs[:, 2 * b + i, :]).then_inc(stat, 1)
                if step == 2:
                    for i in range(2):
                        dve.wait_ge(stat, base + i + 1)
                        nc.vector.bn_aggr(mv[:, b % 2, i, :], stats[:, i, :]).then_inc(stat, 1)

            def tokens_out(b):
                dve.wait_ge(rstd_ready, GROUPS + b + 1)
                if b >= 2:
                    dve.wait_ge(sent[b % 2], 16 * 4 * (b // 2))
                    dve.wait_ge(row1_done, b - 1)
                for i in range(2):
                    c = nc.vector.tensor_scalar(rows[:, b % 2, 0, i, 0:D], xs[:, 2 * b + i, :], mv[:, b % 2, i, 0:1],
                                                rstd[:, b % 2, i:i + 1], ALU.subtract, ALU.mult)
                c.then_inc(h2_ready, 1)

            def top_two(b, step):
                r = S_ROUTE * b
                if step == 0:
                    dve.wait_ge(lg_ready, b + 1)
                    nc.vector.tensor_tensor(lg[:, :, :], LOGITS, bg2[:, :, :], ALU.add).then_inc(route, 1)
                if step == 1:
                    dve.wait_ge(route, r + 1)
                    for t in range(2):
                        c = nc.vector.max(top[:, t, :], lg[:, t, :])
                    c.then_inc(route, 1)
                if step == 2:
                    dve.wait_ge(route, r + 2)
                    for t in range(2):
                        c = nc.vector.max_index(topi[:, t, :], top[:, t, :], lg[:, t, :])
                    c.then_inc(route, 1)
                    nc.vector.tensor_tensor(d01[:, :], top[:, :, 1], top[:, :, 0], ALU.subtract).then_inc(d01_ready, 1)
                if step == 3:
                    dve.wait_ge(route, r + 3)
                    nc.vector.tensor_copy(idxf[:, :].rearrange("p (t k) -> p t k", t=2), topi[:, :, 0:TOPK]
                                          ).then_inc(route, 1)
                if step == 4:
                    dve.wait_ge(route, r + 4)
                    iv = idxf[:, :]
                    nc.vector.tensor_tensor(oh[:, :, :], iotak[:, :, :],
                                            bass.AP(tensor=iv.tensor, offset=iv.offset, ap=[iv.ap[0], [1, 4], [0, E]]),
                                            ALU.is_equal).then_inc(route, 1)
                if step == 5:
                    dve.wait_ge(route, r + 5)
                    ov = oh[:, :, :].rearrange("p (t k) e -> p t k e", k=TOPK)
                    if b >= 2:
                        dve.wait_ge(pos_ready, b - 1)
                    nc.vector.tensor_tensor(lab[:, b % 2, :, :], ov[:, :, 0, :], ov[:, :, 1, :], ALU.add
                                            ).then_inc(lab_ready, 1)
                if step == 6:
                    dve.wait_ge(lab_ready, b + 1)
                    nc.vector.tensor_tensor(run1[:, :], run[:, b % 2, :], lab[:, b % 2, 0, :], ALU.add
                                            ).then_inc(route, 1)
                if step == 7:
                    dve.wait_ge(route, r + 6)
                    if b >= 1:
                        dve.wait_ge(pos_ready, b)
                    nc.vector.tensor_tensor(run[:, (b + 1) % 2, :], run1[:, :], lab[:, b % 2, 1, :], ALU.add
                                            ).then_inc(route, 1)

            def destinations(b, step):
                wr = S_WTS * b
                if step == 0:
                    dve.wait_ge(e01_done, b + 1)
                    nc.vector.tensor_scalar(s01[:, :], e01[:, :], 1.0, None, ALU.add).then_inc(wts_done, 1)
                    for k in range(TOPK):
                        nc.vector.tensor_copy(rows[:, b % 2, k, :, D].bitcast(i32), dest_meta[:, 2 * b:2 * b + 2, k])
                if step == 1:
                    dve.wait_ge(wts_done, wr + 1)
                    nc.vector.reciprocal(rows[:, b % 2, 0, :, D + 1], s01[:, :]).then_inc(wts_done, 1)
                    dve.wait_ge(pos_ready, b + 1)
                    pv = POS
                    nc.vector.tensor_tensor(ohp[:, :, :].rearrange("p (t k) e -> p t k e", k=TOPK),
                                            bass.AP(tensor=pv.tensor, offset=pv.offset,
                                                    ap=[pv.ap[0], [E, 2], [0, TOPK], [1, E]]),
                                            oh[:, :, :].rearrange("p (t k) e -> p t k e", k=TOPK),
                                            ALU.mult).then_inc(wts_done, 1)
                if step == 2:
                    dve.wait_ge(wts_done, wr + 3)
                    nc.vector.tensor_tensor(rows[:, b % 2, 1, :, D + 1], rows[:, b % 2, 0, :, D + 1], e01[:, :], ALU.mult)
                    nc.vector.tensor_reduce(posk[:, :], ohp[:, :, :], axis=AX.X, op=ALU.add).then_inc(wts_done, 1)
                if step == 3:
                    dve.wait_ge(wts_done, wr + 4)
                    nc.vector.tensor_scalar(over[:, :], posk[:, :], float(CAP), float(NEVER), ALU.is_gt, ALU.mult)
                    nc.vector.scalar_tensor_tensor(slotf[:, :], idxf[:, :], float(CAP), posk[:, :], ALU.mult, ALU.add
                                                   ).then_inc(wts_done, 1)
                if step == 4:
                    dve.wait_ge(wts_done, wr + 5)
                    if b >= 2:
                        dve.wait_ge(sent[b % 2], 16 * 4 * (b // 2))
                    nc.vector.scalar_tensor_tensor(dest[:, b % 2, :], slotf[:, :], -1.0, over[:, :], ALU.add, ALU.add
                                                   ).then_inc(dest_ready, 1)

            for U in range(-2, UNITS + 4):
                for step in range(STEPS):
                    if U + 2 < UNITS:
                        maxima(U + 2, step)
                    if 0 <= U - 2 < UNITS:
                        if step == 3:
                            invert(U - 2)
                        if step == 4:
                            normalize(U - 2)
                    if U % 2:
                        if 0 <= (U - 3) // 2 < B and 8 <= step < 11:
                            tokens_norm((U - 3) // 2, step - 8)
                        if 0 <= (U - 5) // 2 < B:
                            if step < 2:
                                top_two((U - 5) // 2, 6 + step)
                            elif step < 7:
                                destinations((U - 5) // 2, step - 2)
                    elif 0 <= (U - 4) // 2 < B:
                        if step == 2:
                            tokens_out((U - 4) // 2)
                        if step >= 6:
                            top_two((U - 4) // 2, step - 6)
                if U + 2 < UNITS:
                    split_maxima(U + 2)

            def gated(e, c):
                n = HC * e + c
                dve.wait_ge(gate_done, n + 1)
                nc.vector.tensor_tensor(hid[:, e % 2, c, :], PS[:, 4 + n % 2, 0:CAP], gate[:, n % 2, :],
                                        ALU.mult).then_inc(hid_done, 1)

            def weighted(e):
                dve.wait_ge(yo_ready, e + 1)
                if e >= 2:
                    dve.wait_ge(answered[e % 2], 16 * ST_TILES * (e // 2))
                for s in range(ST_TILES):
                    n = 128 if s < ST_TILES - 1 else LAST
                    nc.vector.tensor_scalar(yr[0:n, e % 2, s, :], PS[0:n, 6 + e % 2, 128 * s:128 * s + D],
                                            ex[0:n, e, s, D + 1:D + 2], None, ALU.mult).then_inc(yr_done, 1)

            for e in range(E):
                for c in range(HC):
                    gated(e, c)
                    if c == 0 and e >= 1:
                        weighted(e - 1)
            weighted(E - 1)
            for g in range(GROUPS):
                v = yy[:, 0, 4 * g:4 * g + 4, :]
                dve.wait_ge(yy_in[g], 32)
                nc.vector.tensor_tensor(v, v, yy[:, 1, 4 * g:4 * g + 4, :], ALU.add).then_inc(sum_done, 1)
                dve.wait_ge(sum_done, g + 1)
                xv = xs[:, 4 * g:4 * g + 4, :]
                nc.vector.scalar_tensor_tensor(xv, v, tgf[:, 0:1], xv, ALU.mult, ALU.add).then_inc(out_done, 1)

        @block.tensor
        def _(pe):
            def transpose4(src, bank):
                for i in range(4):
                    c = nc.tensor.transpose(PS[:, bank, 128 * i:128 * i + 128], src[:, i, :], ident[:, :])
                c.then_inc(tr_ready, 1)

            pe.wait_ge(consts, 2)
            pe.wait_ge(ctx_in, 16)
            transpose4(ctxs, 0)
            pe.wait_ge(w_in, 48)
            pe.wait_ge(hT_ready, 1)
            nc.tensor.matmul(PS[:, 4, :].rearrange("p (b m) -> p b m", m=M), wks[:, :], ctxT[:, :, 0:M],
                             start=True, stop=True).then_inc(k_ready, 1)
            for b in range(B):
                c = nc.tensor.matmul(PS[:, 6 if b < 4 else 2, 128 * (b % 4):128 * (b % 4) + 128], ctxT[:, b, :],
                                     wvs[:, :], start=True, stop=True)
            c.then_inc(v_ready, 1)
            pe.wait_ge(xn_ready, 1)
            transpose4(xn[0], 1)
            for g in range(GROUPS):
                i = (g + 1) % 2
                if g + 1 < GROUPS:
                    pe.wait_ge(xn_ready, g + 2)
                    pe.wait_ge(hT_ready, g + 1)
                    transpose4(xn[(g + 1) % 2], g % 2)
                pe.wait_ge(hT_ready, g + 2)
                if g == 1:
                    pe.wait_ge(v_done, 1)
                if g >= 2:
                    pe.wait_ge(rq_done, g - 1)
                nc.tensor.matmul(PS[:, 2 + i, :], wqs[:, :], hT[g % 2], start=True, stop=True).then_inc(q_ready, 1)
                if g >= 1:
                    pe.wait_ge(rk_done, g)
                nc.tensor.matmul(PS[:, 4 + i, :], wks[:, :], hT[g % 2], start=True, stop=True).then_inc(k_ready, 1)
                if g >= 1:
                    pe.wait_ge(v_done, g)
                for t in range(4):
                    c = nc.tensor.matmul(PS[:, 6 + i, 128 * t:128 * t + 128], hT[g % 2][:, 128 * t:128 * t + 128],
                                         wvs[:, :], start=True, stop=True)
                c.then_inc(v_ready, 1)

            def scores(U, step):
                s, bb, g0 = place(U)
                g, piece = step // 3, step % 3
                if step == 0 and U % 4 == 0:
                    pe.wait_ge(stack_in[U // 4], 16 * 24)
                    if U // 4 < RING:
                        pe.wait_ge(fixed_in[U // 4], 16 * 3)
                n = STEPS * U + step
                if n >= 3:
                    pe.wait_ge(max_done, n - 2)
                bank = PS[:, S_BANKS[n % 3], :]
                if piece == 0:
                    q = qst[0:MROW, s, g0 + g, bb, 0:128]
                    nc.tensor.matmul(bank[:, 0:128], q, kst[0:MROW, s, g0 + g, bb, 0:128], start=True, stop=False)
                    nc.tensor.matmul(bank[:, 128:384], q, kst[0:MROW, s, g0 + g, bb, N:2 * N],
                                     start=False, stop=False)
                    c = nc.tensor.matmul(bank[:, 0:512].rearrange("p (q k) -> p q k", q=2)[:, :, 0:128],
                                         identb[:, :], maskb[:, :, :], start=False, stop=True)
                else:
                    par = piece - 1
                    own = 128 + M * par
                    nc.tensor.matmul(bank[:, 0:KEYS], qst[0:MROW, s, g0 + g, bb, 128:256],
                                     kst[0:MROW, s, g0 + g, bb, KEYS * par:KEYS * (par + 1)],
                                     start=True, stop=False)
                    c = nc.tensor.matmul(bank[:, own:own + 128], identb[:, :], maskb[:, 0, :],
                                         start=False, stop=True)
                c.then_inc(s_ready, 1)

            def scores_t(U, g, par):
                s, bb, g0 = place(U)
                if g == 0 and par == 0:
                    pe.wait_ge(m_in[U % 2], 64 * (U // 2 + 1))
                q = qst[0:KROWS, s, g0 + g, bb, :]
                k = kst[0:KROWS, s, g0 + g, bb, :]
                odd = N + 2 * M
                k0 = odd * par
                n = 2 * (UP * U + g) + par
                if n >= 2:
                    pe.wait_ge(exp_done, n - 1)
                nc.tensor.matmul(PS[:, n % 2, 0:N], k[:, k0:k0 + 128], q, start=True, stop=True)
                nc.tensor.matmul(PS[:, n % 2, N:N + 128], k[:, k0 + 128:k0 + N], q[:, 128:N],
                                 start=True, stop=True)
                nc.tensor.matmul(PS[:, n % 2, N + 128:2 * N], k[:, N:odd], q[:, 128 * par:128 * par + 128],
                                 start=True, stop=True).then_inc(st_ready, 1)

            def values(V, chunk):
                b, g0 = V // 2, UP * (V % 2)
                if chunk == 0:
                    pe.wait_ge(exp_done, 2 * UP * (V + 1))
                    pe.wait_ge(vp_ready, b + 1)
                    if V >= 1:
                        pe.wait_ge(ot_done, V)
                if chunk == 1:
                    pe.wait_ge(sel_done, UP * V + UP)
                for par in {0: (None,), 1: (0,), 2: (1,), 3: (0, 1)}[chunk]:
                    for j in range(UP):
                        w = pt[:, V % 2, j, :].rearrange("p (e c) -> p e c", e=2)
                        if chunk == 0:
                            blk, q0, w = g0 + j, 0, w[:, :, N + 128:2 * N]
                        elif chunk < 3:
                            blk, q0, w = PAIRS + 2 * (g0 + j) + par, 0, w[:, par, 0:N]
                        else:
                            blk, q0, w = 3 * PAIRS + 2 * (g0 + j) + par, 128, w[:, par, N:N + 128]
                        c = nc.tensor.matmul(O[VW * j:VW * j + VW, q0:N], vp[:, b % 2, blk, :], w,
                                             start=(chunk == 0), stop=(chunk == 3 and par == 1))
                if chunk == 3:
                    c.then_inc(pv_done, 1)

            def maxima_t(U):
                pe.wait_ge(split_done, 2 * (U + 1))
                if U >= 1:
                    pe.wait_ge(mrow_done, U)
                if U >= 4:
                    pe.wait_ge(att_done, U - 3)
                for t in range(2):
                    c = nc.tensor.matmul(MT[:, 128 * t:128 * t + 128],
                                         mxb[:, U % 2, t, :, :].rearrange("p c r -> p (c r)"), identb[:, :],
                                         start=True, stop=True)
                c.then_inc(mT_ready, 1)

            def turn_values(V):
                pe.wait_ge(ot_done, V + 1)
                if V + 3 < UNITS:
                    pe.wait_ge(mrow_done, V + 4)
                if V >= 1:
                    pe.wait_ge(att_done, V)
                for t in range(2):
                    c = nc.tensor.transpose(PS[:, 7, 128 * t:128 * t + 128], ots[:, V % 2, 128 * t:128 * t + 128],
                                            ident[:, :])
                c.then_inc(oT_ready, 1)

            def turn_attention(b):
                pe.wait_ge(att_done, 2 * b + 2)
                if b >= 1:
                    pe.wait_ge(wts_done, S_WTS * (b - 1) + 3)
                for t in range(2):
                    c = nc.tensor.transpose(MISC[:, 128 * t:128 * t + 128], att[:, b % 2, t, :], ident[:, :])
                c.then_inc(attT_ready, 1)

            def project(b):
                pe.wait_ge(attT_done, b + 1)
                if b == 0:
                    pe.wait_ge(tanh_done, 1)
                for t in range(2):
                    nc.tensor.matmul(MISC[:, 128 * t:128 * t + 128], attT[:, 128 * t:128 * t + 128], wos[:, :],
                                     start=True, stop=False)
                    c = nc.tensor.matmul(MISC[:, 128 * t:128 * t + 128], onesf[:, :], bos[:, :],
                                         start=False, stop=True)
                c.then_inc(y_ready, 1)

            def turn_tokens(b):
                pe.wait_ge(h2_ready, b + 1)
                for t in range(2):
                    c = nc.tensor.transpose(MISC[:, 128 * t:128 * t + 128], rows[:, b % 2, 0, t, 0:D], ident[:, :])
                c.then_inc(h2T_ready, 1)

            def logits(b):
                pe.wait_ge(h2T_done, b + 1)
                for t in range(2):
                    c = nc.tensor.matmul(LOGITS[:, t, :], h2t[:, 128 * t:128 * t + 128], wgs[:, :],
                                         start=True, stop=True)
                c.then_inc(lg_ready, 1)

            def positions(b):
                pe.wait_ge(lab_ready, b + 1)
                pe.wait_ge(route, S_ROUTE * b)
                cur, rn = lab[:, b % 2, :, :], run[:, b % 2, :]
                nc.tensor.matmul(POS[:, 0, :], tri[:, :], cur[:, 0, :], start=True, stop=False)
                nc.tensor.matmul(POS[:, 0, :], ones[:, :], rn, start=False, stop=True)
                nc.tensor.matmul(POS[:, 1, :], tri[:, :], cur[:, 1, :], start=True, stop=False)
                nc.tensor.matmul(POS[:, 1, :], ones[:, :], cur[:, 0, :], start=False, stop=False)
                nc.tensor.matmul(POS[:, 1, :], ones[:, :], rn, start=False, stop=True).then_inc(pos_ready, 1)

            pe.wait_ge(consts, 13)
            pe.wait_ge(cast, 4)
            pe.wait_ge(rq_done, GROUPS)
            pe.wait_ge(rk_done, GROUPS + 1)
            pe.wait_ge(v_done, GROUPS + 1)
            for U in range(-2, UNITS + 4):
                for step in range(STEPS):
                    if U + 2 < UNITS:
                        scores(U + 2, step)
                    if step == 1 and -1 <= U and U + 1 < UNITS:
                        maxima_t(U + 1)
                    if step == 3 and 0 <= U - 2 < UNITS:
                        turn_values(U - 2)
                    if U % 2 and 0 <= (U - 3) // 2 < B:
                        if step == 6:
                            turn_attention((U - 3) // 2)
                        if step == 8:
                            project((U - 3) // 2)
                    if U % 2 == 0 and 0 <= (U - 4) // 2 < B:
                        if step == 4:
                            turn_tokens((U - 4) // 2)
                        if step == 6:
                            logits((U - 4) // 2)
                    if U % 2 and step == 1 and 0 <= (U - 5) // 2 < B:
                        positions((U - 5) // 2)
                    if step % 3 < 2:
                        if 0 <= U < UNITS:
                            scores_t(U, step // 3, step % 3)
                    elif 0 <= U - 1 < UNITS:
                        values(U - 1, step // 3)

            def turn(e):
                pe.wait_ge(ex_in[e], 32)
                if e >= 2:
                    pe.wait_ge(xT_done, e - 1)
                for s in range(ST_TILES):
                    n = 128 if s < ST_TILES - 1 else LAST
                    c = nc.tensor.transpose(PS[:, e % 2, 128 * s:128 * s + n], ex[0:n, e, s, 0:D], ident[0:n, 0:n])
                c.then_inc(xT_ready, 1)

            def up(e, c):
                if c == 0:
                    pe.wait_ge(wx_in[e % 2], 32 * (e // 2 + 1))
                    pe.wait_ge(xT_done, e + 1)
                n = HC * e + c
                if n >= 2:
                    pe.wait_ge(hid_done, n - 1)
                nc.tensor.matmul(PS[:, 2 + n % 2, 0:CAP], w1s[:, e % 2, 128 * c:128 * c + 128], xT[:, e % 2, :],
                                 start=True, stop=True)
                nc.tensor.matmul(PS[:, 4 + n % 2, 0:CAP], w2s[:, e % 2, 128 * c:128 * c + 128], xT[:, e % 2, :],
                                 start=True, stop=True).then_inc(h_ready, 1)

            def down(e):
                pe.wait_ge(w3_in[e % 2], 16 * (e // 2 + 1))
                pe.wait_ge(hid_done, HC * (e + 1))
                if e >= 2:
                    pe.wait_ge(yr_done, ST_TILES * (e - 1))
                for s in range(ST_TILES):
                    n = 128 if s < ST_TILES - 1 else LAST
                    for c in range(HC):
                        m = nc.tensor.matmul(PS[0:n, 6 + e % 2, 128 * s:128 * s + D],
                                             hid[:, e % 2, c, 128 * s:128 * s + n], w3s[:, e % 2, c, :],
                                             start=(c == 0), stop=(c == HC - 1))
                m.then_inc(yo_ready, 1)

            turn(0)
            up(0, 0)
            for e in range(E):
                for c in range(1, HC):
                    if c == HC - 1 and e + 1 < E:
                        turn(e + 1)
                    up(e, c)
                if e + 1 < E:
                    up(e + 1, 0)
                down(e)
    return nc


def x_tiles(ap):
    return ap.rearrange("b (t p) d -> p (b t) d", p=128)


def kernel(x, ctx_1024, g_xattn, g_ffn, L0_xattn_Wq, L0_xattn_Wkv, L0_xattn_Wout, L0_xattn_bout,
           L0_ffn_Wg, L0_ffn_bg, L0_ffn_W1, L0_ffn_W2, L0_ffn_W3):
    import numpy as _np
    import concourse.bacc as _bacc
    from concourse import mybir as _mybir
    from concourse.bass_utils import run_bass_kernel_spmd as _run

    def by_parity(w):
        return _np.asarray(w).reshape(128, 8, 2, 8).transpose(0, 2, 3, 1).reshape(128, 128)

    wkv = _np.asarray(L0_xattn_Wkv)
    ins = {"x": x, "ctx": ctx_1024, "g_xattn": g_xattn, "g_ffn": g_ffn, "wq": by_parity(L0_xattn_Wq),
           "wk": by_parity(wkv[:, :128]), "wv": wkv[:, 128:], "wout": L0_xattn_Wout, "bout": L0_xattn_bout,
           "wg": L0_ffn_Wg, "bg": L0_ffn_bg, "w1": L0_ffn_W1, "w2": L0_ffn_W2, "w3": L0_ffn_W3}
    nc = _bacc.Bacc("TRN2", target_bir_lowering=False, num_devices=1)
    arrays, args = {}, {}
    for name, a in ins.items():
        a = _np.ascontiguousarray(a)
        arrays[f"in_{name}"] = a
        args[name] = nc.dram_tensor(f"in_{name}", a.shape, _mybir.dt.from_np(a.dtype), kind="ExternalInput").ap()
    fp32 = _mybir.dt.float32
    args["slots_dram"] = nc.dram_tensor("slots", (8 * 320, 130), fp32, kind="Internal").ap()
    args["answers_dram"] = nc.dram_tensor("answers", (2 * 2048, 128), fp32, kind="Internal").ap()
    args["out"] = nc.dram_tensor("out_0", (8, 256, 128), fp32, kind="ExternalOutput").ap()
    flamingo_gated_block(nc, **args)
    r = _run(nc, [arrays], core_ids=[0])
    return r.results[0]["out_0"]
```
